# Optimizing a Trainium2 kernel written in Bass

```python
import numpy as np
import jax
import jax.numpy as jnp

def _softmax(x, axis=-1):
    return jax.nn.softmax(x, axis=axis)

def _gelu(x):
    return jax.nn.gelu(x, approximate=True)

def _silu(x):
    return jax.nn.silu(x)

def _sigmoid(x):
    return jax.nn.sigmoid(x)

def _layernorm(x, axis=-1, eps=1e-05):
    m = jnp.mean(x, axis=axis, keepdims=True)
    v = jnp.var(x, axis=axis, keepdims=True)
    return (x - m) / jnp.sqrt(v + eps)

def _scatter_add(tgt, idx, src, axis=0):
    return tgt.at[idx].add(src)

def _segment_sum(src, seg, n):
    return jax.ops.segment_sum(src, seg, n)
kernel_name = 'mk_prb_d1_jaxref_r8_7f5ccd'

def setup_inputs(seed: int=0):
    np.random.seed(seed)
    _w = jnp.asarray

    def _L0_attn_setup():
        import jax, jax.numpy as jnp
        import numpy as np
        H = 512
        D = 1024
        N = 16
        K = 4
        R = 32
        BATCH = 1
        L = 256
        EPS = 1e-06

        def _rmsnorm(x, w):
            return x * jax.lax.rsqrt(jnp.mean(x * x, axis=-1, keepdims=True) + EPS) * w
        key = jax.random.key(seed)
        ks = jax.random.split(key, 10)
        s = 0.02
        return {'hidden_states': jax.random.normal(ks[0], (BATCH, L, H), jnp.float32), 'W_in': jax.random.normal(ks[1], (2 * D, H), jnp.float32) * s, 'conv_w': jax.random.normal(ks[2], (D, K), jnp.float32) * s, 'conv_b': jax.random.normal(ks[3], (D,), jnp.float32) * s, 'Wx': jax.random.normal(ks[4], (R + 2 * N, D), jnp.float32) * s, 'dt_ln_w': jnp.ones((R,), jnp.float32), 'b_ln_w': jnp.ones((N,), jnp.float32), 'c_ln_w': jnp.ones((N,), jnp.float32), 'Wdt': jax.random.normal(ks[5], (D, R), jnp.float32) * s, 'dt_bias': jax.random.normal(ks[6], (D,), jnp.float32) * s, 'A': -jnp.exp(jax.random.normal(ks[7], (D, N), jnp.float32) * 0.5), 'D_param': jnp.ones((D,), jnp.float32), 'W_out': jax.random.normal(ks[8], (H, D), jnp.float32) * s}
    _L0_attn_in = _L0_attn_setup()

    def _L0_ffn_setup():
        import jax, jax.numpy as jnp
        import numpy as np
        HD, M = (512, 1792)
        key = jax.random.key(seed)
        k_x, k_g, k_u, k_d = jax.random.split(key, 4)
        scale = 1.0 / np.sqrt(HD)
        x = jax.random.normal(k_x, (4, 256, HD), dtype=jnp.float16)
        W_gate = jax.random.normal(k_g, (M, HD), dtype=jnp.float16) * jnp.float16(scale)
        W_up = jax.random.normal(k_u, (M, HD), dtype=jnp.float16) * jnp.float16(scale)
        W_down = jax.random.normal(k_d, (HD, M), dtype=jnp.float16) * jnp.float16(1.0 / np.sqrt(M))
        return {'x': x, 'W_gate': W_gate, 'W_up': W_up, 'W_down': W_down}
    _L0_ffn_in = _L0_ffn_setup()
    _d = {'L0_attn_hidden_states': _L0_attn_in['hidden_states'], 'L0_attn_W_in': _L0_attn_in['W_in'], 'L0_attn_conv_w': _L0_attn_in['conv_w'], 'L0_attn_conv_b': _L0_attn_in['conv_b'], 'L0_attn_Wx': _L0_attn_in['Wx'], 'L0_attn_dt_ln_w': _L0_attn_in['dt_ln_w'], 'L0_attn_b_ln_w': _L0_attn_in['b_ln_w'], 'L0_attn_c_ln_w': _L0_attn_in['c_ln_w'], 'L0_attn_Wdt': _L0_attn_in['Wdt'], 'L0_attn_dt_bias': _L0_attn_in['dt_bias'], 'L0_attn_A': _L0_attn_in['A'], 'L0_attn_D_param': _L0_attn_in['D_param'], 'L0_attn_W_out': _L0_attn_in['W_out'], 'L0_ffn_W_gate': _L0_ffn_in['W_gate'], 'L0_ffn_W_up': _L0_ffn_in['W_up'], 'L0_ffn_W_down': _L0_ffn_in['W_down']}
    _x0 = _d['L0_attn_hidden_states']
    _d['L0_attn_hidden_states'] = jax.random.normal(jax.random.fold_in(jax.random.key(seed), 1), (2, 1024, 512), dtype=_x0.dtype)
    del _x0
    return _d

def reference(L0_attn_hidden_states, L0_attn_W_in, L0_attn_conv_w, L0_attn_conv_b, L0_attn_Wx, L0_attn_dt_ln_w, L0_attn_b_ln_w, L0_attn_c_ln_w, L0_attn_Wdt, L0_attn_dt_bias, L0_attn_A, L0_attn_D_param, L0_attn_W_out, L0_ffn_W_gate, L0_ffn_W_up, L0_ffn_W_down):

    def _L0_attn_ref(hidden_states, W_in, conv_w, conv_b, Wx, dt_ln_w, b_ln_w, c_ln_w, Wdt, dt_bias, A, D_param, W_out):
        import jax, jax.numpy as jnp
        import numpy as np
        H = 512
        D = 1024
        N = 16
        K = 4
        R = 32
        BATCH = 1
        L = 256
        EPS = 1e-06

        def _rmsnorm(x, w):
            return x * jax.lax.rsqrt(jnp.mean(x * x, axis=-1, keepdims=True) + EPS) * w
        proj = hidden_states @ W_in.T
        u, gate = jnp.split(proj, 2, axis=-1)
        x = jnp.transpose(u, (0, 2, 1))
        x = jax.lax.conv_general_dilated(x, conv_w[:, None, :], window_strides=(1,), padding=[(K - 1, 0)], dimension_numbers=('NCH', 'OIH', 'NCH'), feature_group_count=D)
        u = jax.nn.silu(jnp.transpose(x, (0, 2, 1)) + conv_b)
        ssm_p = u @ Wx.T
        dt, Bm, Cm = jnp.split(ssm_p, [R, R + N], axis=-1)
        dt = _rmsnorm(dt, dt_ln_w)
        Bm = _rmsnorm(Bm, b_ln_w)
        Cm = _rmsnorm(Cm, c_ln_w)
        delta = jax.nn.softplus(dt @ Wdt.T + dt_bias)

        def step(state, xs):
            d_t, B_t, C_t, u_t = xs
            dA = jnp.exp(d_t[..., None] * A)
            state = dA * state + (d_t * u_t)[..., None] * B_t[:, None, :]
            y_t = jnp.einsum('bdn,bn->bd', state, C_t)
            return (state, y_t)
        init = jnp.zeros((hidden_states.shape[0], D, N), hidden_states.dtype)
        xs = (jnp.swapaxes(delta, 0, 1), jnp.swapaxes(Bm, 0, 1), jnp.swapaxes(Cm, 0, 1), jnp.swapaxes(u, 0, 1))
        _, ys = jax.lax.scan(step, init, xs)
        y = jnp.swapaxes(ys, 0, 1) + u * D_param
        y = y * jax.nn.silu(gate)
        return y @ W_out.T

    def _L0_ffn_ref(x, W_gate, W_up, W_down):
        import jax, jax.numpy as jnp
        import numpy as np
        HD, M = (512, 1792)
        gate = jnp.einsum('bsh,mh->bsm', x, W_gate)
        up = jnp.einsum('bsh,mh->bsm', x, W_up)
        h = jax.nn.silu(gate) * up
        out = jnp.einsum('bsm,hm->bsh', h, W_down)
        return out
    x = L0_attn_hidden_states
    xn = _layernorm(x, axis=-1)
    x = x + _L0_attn_ref(xn, L0_attn_W_in, L0_attn_conv_w, L0_attn_conv_b, L0_attn_Wx, L0_attn_dt_ln_w, L0_attn_b_ln_w, L0_attn_c_ln_w, L0_attn_Wdt, L0_attn_dt_bias, L0_attn_A, L0_attn_D_param, L0_attn_W_out) + _L0_ffn_ref(xn, L0_ffn_W_gate, L0_ffn_W_up, L0_ffn_W_down)
    return x

_drawn_inputs = setup_inputs


def setup_inputs(seed=0):
    import zlib

    import numpy as np

    out = dict(_drawn_inputs(seed))
    spreads = {'L0_attn_dt_ln_w': (1.0, 0.6),
     'L0_attn_b_ln_w': (1.0, 0.6),
     'L0_attn_c_ln_w': (1.0, 0.6),
     'L0_attn_D_param': (1.0, 0.6)}
    factors = {'L0_attn_W_in': 6.037,
     'L0_attn_conv_w': 6.165,
     'L0_attn_conv_b': 5.093,
     'L0_attn_Wx': 5.766,
     'L0_attn_Wdt': 8.0,
     'L0_attn_dt_bias': 8.0,
     'L0_attn_A': 8.0,
     'L0_attn_W_out': 5.241,
     'L0_ffn_W_gate': 3.441,
     'L0_ffn_W_up': 3.234,
     'L0_ffn_W_down': 3.234}
    for name, (base, spread) in spreads.items():
        noise = np.random.default_rng([zlib.crc32(name.encode()), seed]).standard_normal(out[name].shape)
        drawn = base * np.exp(spread * noise) if base else spread * noise
        out[name] = jnp.asarray(drawn.astype(out[name].dtype))
    for name, factor in factors.items():
        out[name] = (out[name] * factor).astype(out[name].dtype)
    return out
```

```python
from contextlib import ExitStack

import concourse.bass as bass
from concourse import mybir

F32 = mybir.dt.float32
F32R = mybir.dt.float32r
F16 = mybir.dt.float16
ALU = mybir.AluOpType
ACT = mybir.ActivationFunctionType
AX = mybir.AxisListType

P = 128
BATCH, SEQ, H = 2, 1024, 512
D, N, TAPS, R = 1024, 16, 4, 32
M = 1792
T = 512
HALVES = SEQ // T
CHUNKS = BATCH * HALVES
TT = T // P
HT = H // P
DT = D // P
MT = M // P
G = 2
GQ = DT // G
S = 2
ST = T // S
SB = ST // P
W = 2
K = MT // W
LN_EPS, RMS_EPS = 1e-5, 1e-6
SSM = R + 2 * N


def build(nc, x, w_in, conv_w, conv_b, w_x, dt_ln, b_ln, c_ln, w_dt, dt_bias, a_mat, d_par, w_out, w_gu, w_dn,
          b_rows, out):
    with ExitStack() as ctx:
        def sb(name, shape, dt=F32):
            return ctx.enter_context(nc.sbuf_tensor(name, shape, dt))

        def bank(name):
            return ctx.enter_context(nc.psum_tensor(name, [P, 512], F32))

        def sem(name):
            return ctx.enter_context(nc.semaphore(name))

        wdn = sb("wdn", [P, MT, H], F32R)
        wx = sb("wx", [P, DT, SSM])
        wdt = sb("wdt", [R, D])
        cw = sb("cw", [P, DT, TAPS])
        cb = sb("cb", [P, DT])
        dtb = sb("dtb", [P, DT])
        dpar = sb("dpar", [P, DT])
        amat = sb("amat", [P, DT, N])
        lnw = sb("lnw", [P, SSM])
        ident = sb("ident", [P, P])
        minus_half = sb("minus_half", [P, TT * 3])
        win = sb("win", [P, 2, 2, HT, P])
        wgu = sb("wgu", [P, W, 2, HT, P], F16)
        wout = sb("wout", [P, 2, H])
        brow = sb("brow", [P, 2, T])
        acc = sb("acc", [P, TT, H])
        xhi = sb("xhi", [P, HT, T], F16)
        xlo = sb("xlo", [P, HT, T], F16)
        u = sb("u", [P, DT, T])
        gate = sb("gate", [P, DT, T])
        delta = sb("delta", [P, DT, T])
        du = sb("du", [P, DT, T])
        yT = sb("yT", [P, TT, D])
        h = sb("h", [P, G, GQ, T])
        b = sb("b", [P, G, GQ, T])
        state = sb("state", [P, DT, N])
        carry = sb("carry", [P, DT, TAPS - 1])
        stats = sb("stats", [P, TT, 6])
        meanvar = sb("meanvar", [P, TT, 2])
        veps = sb("veps", [P, TT])
        rstd = sb("rstd", [P, TT])
        ss = sb("ss", [P, TT, SSM])
        sq = sb("sq", [P, TT, SSM])
        sw = sb("sw", [P, TT, SSM])
        ssn = sb("ssn", [P, TT, SSM])
        ms = sb("ms", [P, TT, 3])
        mse = sb("mse", [P, TT, 3])
        rms = sb("rms", [P, TT, 3])
        th = sb("th", [P, W, ST])
        v = sb("v", [P, W, ST])
        hf = sb("hf", [P, W, ST])
        hhi = sb("hhi", [P, W, ST], F32R)
        hlo = sb("hlo", [P, W, ST], F32R)
        xn = h[:, 0]
        xnT = h[:, 1]
        pre = b[:, :, :, :].rearrange("p g q t -> p (g q t)")
        UP = T + TAPS - 1
        upad = [pre[:, i * 516:i * 516 + UP] for i in range(2)]
        conv = [pre[:, 1032 + i * T:1032 + (i + 1) * T] for i in range(2)]
        ssT = pre[0:SSM, 2056:2056 + T]
        dtB = pre[0:R + N, 2568:2568 + T]
        y1 = [pre[:, i * T:(i + 1) * T] for i in range(2)]
        y2 = [pre[:, (2 + i) * T:(3 + i) * T] for i in range(2)]
        wdn16 = yT[:, :, :].rearrange("p t d -> p (t d)").bitcast(F16)[:, 0:MT * H]

        pA = [bank(f"pA{i}") for i in range(2)]
        pT = [bank(f"pT{i}") for i in range(2)]
        pG = [bank(f"pG{i}") for i in range(2)]
        pO = [bank(f"pO{i}") for i in range(2)]

        s_const, s_wdn16, s_x, s_brow = (sem(n) for n in ("consts_in", "wdn16_in", "x_in", "brow_in"))
        s_win, s_gu, s_wo = ([sem(f"{n}{i}") for i in range(2)] for n in ("win_in", "gu_in", "wout_in"))
        s_brows, s_out = sem("b_rows_stored"), sem("out_stored")
        s_id0, s_ident, s_half, s_wdn = sem("ident_zero"), sem("ident_done"), sem("half_done"), sem("wdn_done")
        s_passed = sem("passed")
        s_zero, s_fresh = sem("yT_zero"), sem("carry_zero")
        s_stats, s_mv, s_veps, s_rstd, s_xn = (sem(n) for n in ("stats", "meanvar", "veps", "rstd", "xn"))
        s_xT, s_xcopy, s_xlo = sem("x_turned"), sem("x_copied"), sem("x_low")
        s_inproj, s_head, s_upad, s_tap, s_gate, s_conv, s_tail, s_u = (sem(n) for n in (
            "inproj", "upad_head", "upad_tile", "last_tap", "gate_done", "conv_done", "carry_kept", "u_done"))
        s_ssm, s_ssT, s_ssN, s_ss, s_ms, s_mse, s_rms, s_sw, s_ssn = (sem(n) for n in (
            "ssm", "ssT", "ss_turned", "ss", "mean_squares", "ms_eps", "rms", "ss_weighted", "ss_normed"))
        s_dtT, s_dtB = sem("dtB_turned"), sem("dtB")
        s_z, s_abs, s_relu, s_soft, s_delta, s_du = (sem(n) for n in (
            "z", "z_abs", "z_relu", "soft", "delta", "du"))
        s_b, s_state, s_exp, s_scan, s_hT, s_stt = (sem(n) for n in (
            "b_done", "state_kept", "exp_done", "scan_done", "h_turned", "y_added"))
        s_up, s_tanh, s_v, s_hf, s_hhi, s_hlo, s_down, s_ffn = (sem(n) for n in (
            "up_done", "tanh_done", "v_done", "hf_done", "hhi_done", "hlo_done", "down_done", "ffn_added"))
        s_yT, s_y1, s_y2, s_wout, s_final = (sem(n) for n in (
            "y_turned", "y_skip", "y_gated", "outproj", "final"))

        B0, SCAN0, STT0, FFN0, ONE = 2 * G, 2, 2, W, 1

        def per_chunk(c, count, i):
            return c * count + (i + 1)

        def per_n(c, n, count, i):
            return (c * N + n) * count + (i + 1)

        def unit(c, it, w):
            return c * (S * MT) + it * W + (w + 1)

        def states(c, bt, n, g):
            return per_n(c, n, G, g) + (bt + 1) + ONE

        def chunk_loops(eng, chunk, start=None):
            with eng.Fori(0, BATCH) as bt:
                if start:
                    start(bt)
                with eng.Fori(0, HALVES) as half:
                    chunk(bt * HALVES + half, bt)

        def scan_loops(step, after, eng):
            with eng.Fori(0, S) as s:
                step(s * K, s, 0, True, False)
                with eng.Fori(1, K - 1) as k:
                    step(s * K + k, s, k, False, False)
                step(s * K + (K - 1), s, K - 1, False, True)
                if after:
                    after(s)
            for n in range(S * K, N):
                step(n, None, None, False, False)

        def plain(eng):
            eng.sem_inc(s_passed, 1)

        ds = bass.ds
        consts = [(wx[:], w_x), (wdt[:], w_dt), (cw[:], conv_w), (cb[:], conv_b), (dtb[:], dt_bias),
                  (dpar[:], d_par), (amat[:], a_mat), (lnw[:, 0:R], dt_ln.partition_broadcast(P)),
                  (lnw[:, R:R + N], b_ln.partition_broadcast(P)), (lnw[:, R + N:SSM], c_ln.partition_broadcast(P))]
        block = ctx.enter_context(nc.Block())

        @block.sync
        def _(sp):
            sp.sem_inc(s_brow, 16)
            sp.dma_start(wdn16, w_dn).then_inc(s_wdn16, 16)
            for tile, dram in consts:
                sp.dma_start(tile, dram).then_inc(s_const, 16)

            def chunk(c, bt):
                sp.dma_start(acc[:], x[c]).then_inc(s_x, 16)
                for j in range(DT):
                    if j >= 2:
                        sp.wait_ge(s_inproj, per_chunk(c, DT, j - 2))
                    sp.dma_start(win[:, j % 2], w_in[j]).then_inc(s_win[j % 2], 16)
                for j in range(2):
                    sp.dma_start(wout[:, j], w_out[j]).then_inc(s_wo[j], 16)
                sp.wait_ge(s_dtB, c + 1)
                sp.dma_start(b_rows[c], dtB[R:R + N, :]).then_inc(s_brows, 16)
                sp.wait_ge(s_brows, (c + 1) * 16)
                plain(sp)

                def step(n, s, k, first, last):
                    sp.wait_ge(s_b, per_n(c, n, G, -G - 1) + B0)
                    plain(sp)
                    sp.wait_ge(s_brow, per_n(c, n, 1, -1) * 16 + 16)
                    plain(sp)
                    sp.dma_start(brow[:, n % 2, :], b_rows[c, n].partition_broadcast(P)).then_inc(s_brow, 16)
                    if s is not None:
                        for w in range(W):
                            sp.wait_ge(s_up, unit(c, n, w) - W + FFN0)
                            sp.dma_start(wgu[:, w], w_gu[k * W + w]).then_inc(s_gu[w], 16)
                scan_loops(step, None, sp)
                for j in range(2, DT):
                    sp.wait_ge(s_wout, per_chunk(c, DT, j - 2))
                    sp.dma_start(wout[:, j % 2], w_out[j]).then_inc(s_wo[j % 2], 16)
                sp.wait_ge(s_final, (c + 1) * TT)
                sp.dma_start(out[c], acc[:]).then_inc(s_out, 16)
                sp.wait_ge(s_out, (c + 1) * 16)
                plain(sp)
            chunk_loops(sp, chunk)

        @block.gpsimd
        def _(pool):
            pool.sem_inc(s_b, B0)
            pool.sem_inc(s_state, ONE)
            pool.sem_inc(s_tail, ONE)
            pool.memset(ident[:], 0.0).then_inc(s_id0, 1)
            pool.memset(minus_half[:], -0.5).then_inc(s_half, 1)
            pool.wait_ge(s_id0, 1)
            pool.affine_select(out=ident[:], in_=ident[:], compare_op=ALU.not_equal, fill=1.0, base=0,
                               pattern=[[-1, P]], channel_multiplier=1).then_inc(s_ident, 1)
            pool.wait_ge(s_half, 1)
            pool.wait_ge(s_wdn, 1)

            def start(bt):
                pool.wait_ge(s_state, bt * (HALVES * N * G + 1) + ONE)
                pool.wait_ge(s_tail, bt * (HALVES * DT) + ONE)
                plain(pool)
                pool.memset(state[:], 0.0).then_inc(s_state, 1)
                pool.memset(carry[:], 0.0).then_inc(s_fresh, 1)

            def chunk(c, bt):
                pool.wait_ge(s_veps, c + 1)
                pool.tensor_tensor(rstd[:], veps[:], minus_half[:, 0:TT], ALU.pow).then_inc(s_rstd, 1)
                pool.memset(yT[:], 0.0).then_inc(s_zero, 1)
                pool.wait_ge(s_fresh, bt + 1)
                pool.wait_ge(s_tail, c * DT + ONE)
                for j in range(DT):
                    if j >= 2:
                        pool.wait_ge(s_conv, per_chunk(c, DT, j - 2) * (TAPS - 1))
                    plain(pool)
                    pool.tensor_copy(upad[j % 2][:, 0:TAPS - 1], carry[:, j]).then_inc(s_head, 1)
                    pool.wait_ge(s_head, per_chunk(c, DT, j))
                    pool.wait_ge(s_upad, per_chunk(c, DT, j))
                    plain(pool)
                    pool.tensor_copy(carry[:, j], upad[j % 2][:, T:UP]).then_inc(s_tail, 1)
                pool.wait_ge(s_mse, (c + 1) * 2)
                pool.tensor_tensor(rms[:].rearrange("p t k -> p (t k)"), mse[:].rearrange("p t k -> p (t k)"),
                                   minus_half[:], ALU.pow).then_inc(s_rms, 1)

                def make_b(n, g):
                    bn = brow[:, n % 2, :].unsqueeze(1).broadcast_to([P, GQ, T])
                    pool.tensor_tensor(b[:, g], du[:, g * GQ:(g + 1) * GQ], bn, ALU.mult).then_inc(s_b, 1)

                pool.wait_ge(s_du, (c + 1) * G)
                pool.wait_ge(s_brow, per_n(c, 0, 1, 0) * 16 + 16)
                for g in range(G):
                    make_b(0, g)

                def step(n, s, k, first, last):
                    more = s is not None or n < N - 1
                    if more:
                        pool.wait_ge(s_brow, per_n(c, n + 1, 1, 0) * 16 + 16)
                    for g in range(G):
                        pool.wait_ge(s_scan, per_n(c, n, DT, g * GQ + GQ - 1) + SCAN0)
                        plain(pool)
                        pool.tensor_copy(state[:, g * GQ:(g + 1) * GQ, ds(n, 1)],
                                         h[:, g, :, T - 1:T]).then_inc(s_state, 1)
                        if more:
                            make_b(n + 1, g)
                scan_loops(step, None, pool)
            chunk_loops(pool, chunk, start)

        @block.scalar
        def _(act):
            act.wait_ge(s_wdn16, 16)
            act.copy(wdn[:].rearrange("p m n -> p (m n)"), wdn16).then_inc(s_wdn, 1)
            act.wait_ge(s_const, 16 * len(consts))

            def chunk(c, bt):
                for k in range(HT):
                    act.wait_ge(s_xT, per_chunk(c, HT, k))
                    act.copy(xnT[:, k], pA[k % 2][:]).then_inc(s_xcopy, 1)
                    act.copy(xhi[:, k], pA[k % 2][:]).then_inc(s_xcopy, 1)

                def silu_u(j):
                    act.wait_ge(s_conv, per_chunk(c, DT, j) * (TAPS - 1))
                    act.activation(u[:, j], conv[j % 2], ACT.Silu).then_inc(s_u, 1)

                for j in range(DT):
                    act.wait_ge(s_inproj, per_chunk(c, DT, j))
                    if j >= 2:
                        act.wait_ge(s_tail, per_chunk(c, DT, j - 2) + ONE)
                        act.wait_ge(s_conv, per_chunk(c, DT, j - 2) * (TAPS - 1))
                        act.wait_ge(s_u, per_chunk(c, DT, j - 2))
                    act.copy(upad[j % 2][:, TAPS - 1:UP], pO[j % 2][:]).then_inc(s_upad, 1)
                    act.activation(conv[j % 2], pO[j % 2][:], ACT.Identity, bias=cb[:, j:j + 1],
                                   scale=cw[:, j, TAPS - 1:TAPS]).then_inc(s_tap, 1)
                    act.activation(gate[:, j], pG[j % 2][:], ACT.Silu).then_inc(s_gate, 1)
                    if j >= 1:
                        silu_u(j - 1)
                silu_u(DT - 1)
                act.wait_ge(s_ssm, c + 1)
                act.copy(ssT, pT[0][0:SSM, :]).then_inc(s_ssT, 1)
                act.wait_ge(s_ssN, c + 1)
                act.copy(ss[:].rearrange("p t k -> p (t k)"), pT[1][:, 0:TT * SSM]).then_inc(s_ss, 1)
                act.activation(sq[:].rearrange("p t k -> p (t k)"), pT[1][:, 0:TT * SSM],
                               ACT.Square).then_inc(s_ss, 1)
                act.wait_ge(s_dtT, c + 1)
                act.copy(dtB, pT[0][0:R + N, :]).then_inc(s_dtB, 1)
                for j in range(DT):
                    act.wait_ge(s_relu, per_chunk(c, DT, j))
                    act.activation(delta[:, j], pA[j % 2][:], ACT.Abs, bias=dtb[:, j:j + 1]).then_inc(s_abs, 1)
                for g in range(G):
                    act.wait_ge(s_abs, per_chunk(c, DT, g * GQ + GQ - 1))
                    act.activation(delta[:, g * GQ:(g + 1) * GQ], delta[:, g * GQ:(g + 1) * GQ], ACT.Exp,
                                   scale=-1.0).then_inc(s_soft, 1)
                for g in range(G):
                    act.wait_ge(s_soft, per_chunk(c, 2 * G, g))
                    act.activation(delta[:, g * GQ:(g + 1) * GQ], delta[:, g * GQ:(g + 1) * GQ], ACT.Ln,
                                   bias=1.0).then_inc(s_soft, 1)
                act.wait_ge(s_delta, (c + 1) * G)

                def step(n, s, k, first, last):
                    for j in range(DT):
                        act.wait_ge(s_scan, per_n(c, n, DT, j - 2) + SCAN0)
                        act.activation(pA[j % 2][:], delta[:, j], ACT.Exp,
                                       scale=amat[:, j, ds(n, 1)]).then_inc(s_exp, 1)
                    if s is not None:
                        for w in range(W):
                            act.wait_ge(s_up, unit(c, n, w) + FFN0)
                            act.activation(th[:, w], pG[w][:, 0:ST], ACT.Tanh, scale=0.5).then_inc(s_tanh, 1)
                        for w in range(W):
                            act.wait_ge(s_hf, unit(c, n, w) + FFN0)
                            act.wait_ge(s_down, unit(c, n, w) - W + FFN0)
                            act.copy(hhi[:, w], hf[:, w]).then_inc(s_hhi, 1)
                scan_loops(step, None, act)
            chunk_loops(act, chunk)

        @block.vector
        def _(dve):
            dve.sem_inc(s_scan, SCAN0)
            dve.sem_inc(s_stt, STT0)
            dve.sem_inc(s_hf, FFN0)
            dve.sem_inc(s_ffn, ONE)
            dve.wait_ge(s_const, 16 * len(consts))

            def chunk(c, bt):
                dve.wait_ge(s_x, (c + 1) * 16)
                for t in range(TT):
                    dve.bn_stats(stats[:, t], acc[:, t]).then_inc(s_stats, 1)
                for t in range(TT):
                    dve.wait_ge(s_stats, per_chunk(c, TT, t))
                    plain(dve)
                    dve.bn_aggr(meanvar[:, t], stats[:, t]).then_inc(s_mv, 1)
                dve.wait_ge(s_mv, (c + 1) * TT)
                dve.tensor_scalar(veps[:], meanvar[:, :, 1], LN_EPS, None, ALU.add).then_inc(s_veps, 1)
                dve.wait_ge(s_rstd, c + 1)
                for t in range(TT):
                    dve.tensor_scalar(xn[:, t], acc[:, t], meanvar[:, t, 0:1], rstd[:, t:t + 1],
                                      ALU.subtract, ALU.mult).then_inc(s_xn, 1)
                for k in range(HT):
                    dve.wait_ge(s_xcopy, per_chunk(c, HT, k) * 2)
                    dve.tensor_tensor(xlo[:, k], xnT[:, k], xhi[:, k], ALU.subtract).then_inc(s_xlo, 1)
                for j in range(DT):
                    dve.wait_ge(s_head, per_chunk(c, DT, j))
                    dve.wait_ge(s_tap, per_chunk(c, DT, j))
                    for i in range(TAPS - 1):
                        if i:
                            dve.wait_ge(s_conv, per_chunk(c, DT, j - 1) * (TAPS - 1) + i)
                        dve.scalar_tensor_tensor(conv[j % 2], upad[j % 2][:, i:i + T], cw[:, j, i:i + 1],
                                                 conv[j % 2], ALU.mult, ALU.add).then_inc(s_conv, 1)
                dve.wait_ge(s_ss, (c + 1) * 2)
                parts = [(0, R), (R, R + N), (R + N, SSM)]
                for i, (lo, hi) in enumerate(parts):
                    dve.tensor_reduce(ms[:, :, i:i + 1], sq[:, :, lo:hi], AX.X, ALU.add).then_inc(s_ms, 1)
                dve.tensor_tensor(sw[:], ss[:], lnw[:].unsqueeze(1).broadcast_to([P, TT, SSM]),
                                  ALU.mult).then_inc(s_sw, 1)
                dve.wait_ge(s_ms, (c + 1) * 3)
                dve.tensor_scalar(mse[:, :, 0:1], ms[:, :, 0:1], 1.0 / R, RMS_EPS, ALU.mult, ALU.add).then_inc(s_mse, 1)
                dve.tensor_scalar(mse[:, :, 1:3], ms[:, :, 1:3], 1.0 / N, RMS_EPS, ALU.mult, ALU.add).then_inc(s_mse, 1)
                dve.wait_ge(s_rms, c + 1)
                dve.wait_ge(s_sw, c + 1)
                for i, (lo, hi) in enumerate(parts):
                    dve.tensor_tensor(ssn[:, :, lo:hi], sw[:, :, lo:hi],
                                      rms[:, :, i:i + 1].broadcast_to([P, TT, hi - lo]), ALU.mult).then_inc(s_ssn, 1)
                for j in range(DT):
                    dve.wait_ge(s_z, per_chunk(c, DT, j))
                    dve.tensor_scalar(du[:, j], pA[j % 2][:], dtb[:, j:j + 1], 0.0, ALU.add, ALU.max).then_inc(s_relu, 1)
                for g in range(G):
                    js = slice(g * GQ, (g + 1) * GQ)
                    dve.wait_ge(s_relu, (c + 1) * DT)
                    dve.wait_ge(s_soft, per_chunk(c, 2 * G, G + g))
                    dve.tensor_tensor(delta[:, js], delta[:, js], du[:, js], ALU.add).then_inc(s_delta, 1)
                    dve.wait_ge(s_delta, per_chunk(c, G, g))
                    dve.tensor_tensor(du[:, js], delta[:, js], u[:, js], ALU.mult).then_inc(s_du, 1)
                dve.wait_ge(s_zero, c + 1)
                plain(dve)

                def scan(n, g):
                    dve.wait_ge(s_b, per_n(c, n, G, g) + B0)
                    dve.wait_ge(s_state, states(c, bt, n, g - G))
                    for q in range(GQ):
                        j = g * GQ + q
                        dve.wait_ge(s_exp, per_n(c, n, DT, j))
                        dve.tensor_tensor_scan(h[:, g, q], pA[j % 2][:], b[:, g, q], state[:, j, ds(n, 1)],
                                               ALU.mult, ALU.add).then_inc(s_scan, 1)

                def add_y(n, g):
                    for t in range(TT):
                        i = g * TT + t
                        dve.wait_ge(s_hT, per_n(c, n, G * TT, i))
                        dve.scalar_tensor_tensor(yT[:, t, g * 512:(g + 1) * 512], pT[i % 2][:],
                                                 ssn[:, t, ds(n + (R + N), 1)], yT[:, t, g * 512:(g + 1) * 512],
                                                 ALU.mult, ALU.add).then_inc(s_stt, 1)

                def step(n, s, k, first, last):
                    for g in range(G):
                        scan(n, g)
                    add_y(n, 0)
                    if s is not None:
                        for w in range(W):
                            dve.wait_ge(s_tanh, unit(c, n, w))
                            dve.scalar_tensor_tensor(v[:, w], th[:, w], 1.0, pG[w][:, ST:2 * ST],
                                                     ALU.add, ALU.mult).then_inc(s_v, 1)
                        for w in range(W):
                            dve.wait_ge(s_v, unit(c, n, w))
                            dve.scalar_tensor_tensor(hf[:, w], pG[w][:, 0:ST], 0.5, v[:, w],
                                                     ALU.mult, ALU.mult).then_inc(s_hf, 1)
                    add_y(n, 1)
                    if s is not None:
                        for w in range(W):
                            dve.wait_ge(s_hhi, unit(c, n, w))
                            dve.tensor_tensor(hlo[:, w], hf[:, w], hhi[:, w].bitcast(F32),
                                              ALU.subtract).then_inc(s_hlo, 1)

                def add_ffn(s):
                    dve.wait_ge(s_down, unit(c, s * K + (K - 1), W - 1) + FFN0)
                    for t in range(SB):
                        dve.tensor_tensor(acc[:, ds(s * SB + t, 1)].squeeze(1), acc[:, ds(s * SB + t, 1)].squeeze(1),
                                          pO[t][:], ALU.add).then_inc(s_ffn, 1)

                scan_loops(step, add_ffn, dve)
                for j in range(DT):
                    dve.wait_ge(s_yT, per_chunk(c, DT, j))
                    dve.scalar_tensor_tensor(y1[j % 2], u[:, j], dpar[:, j:j + 1], pT[j % 2][:],
                                             ALU.mult, ALU.add).then_inc(s_y1, 1)
                    dve.wait_ge(s_y1, per_chunk(c, DT, j))
                    if j >= 2:
                        dve.wait_ge(s_wout, per_chunk(c, DT, j - 2))
                    dve.tensor_tensor(y2[j % 2], y1[j % 2], gate[:, j], ALU.mult).then_inc(s_y2, 1)
                dve.wait_ge(s_wout, (c + 1) * DT)
                dve.wait_ge(s_ffn, (c + 1) * S * SB + ONE)
                for t in range(TT):
                    dve.tensor_tensor(acc[:, t], acc[:, t], (pO + pA)[t][:], ALU.add).then_inc(s_final, 1)
            chunk_loops(dve, chunk)

        @block.tensor
        def _(pe):
            pe.sem_inc(s_up, FFN0)
            pe.sem_inc(s_down, FFN0)
            pe.wait_ge(s_const, 16 * len(consts))
            pe.wait_ge(s_ident, 1)
            pe.wait_ge(s_wdn, 1)

            def chunk(c, bt):
                pe.wait_ge(s_xn, (c + 1) * TT)
                for k in range(HT):
                    if k >= 2:
                        pe.wait_ge(s_xcopy, per_chunk(c, HT, k - 2) * 2)
                    for t in range(TT):
                        last = pe.transpose(pA[k % 2][:, t * P:(t + 1) * P], xn[:, t, k * P:(k + 1) * P], ident[:])
                    last.then_inc(s_xT, 1)
                pe.wait_ge(s_xcopy, (c + 1) * HT * 2)

                def ssm(j):
                    pe.wait_ge(s_u, per_chunk(c, DT, j))
                    return pe.matmul(pT[0][0:SSM, :], wx[:, j], u[:, j], start=(j == 0), stop=(j == DT - 1))

                for j in range(DT):
                    pe.wait_ge(s_win[j % 2], per_chunk(c, DT // 2, j // 2) * 16)
                    if j >= 2:
                        pe.wait_ge(s_gate, per_chunk(c, DT, j - 2))
                        pe.wait_ge(s_tap, per_chunk(c, DT, j - 2))
                    for part, bank_ in ((0, pO[j % 2]), (1, pG[j % 2])):
                        for k in range(HT):
                            last = pe.matmul(bank_[:], win[:, j % 2, part, k], xnT[:, k],
                                             start=(k == 0), stop=(k == HT - 1))
                    last.then_inc(s_inproj, 1)
                    if j >= 2:
                        ssm(j - 2)
                ssm(DT - 2)
                ssm(DT - 1).then_inc(s_ssm, 1)
                pe.wait_ge(s_ssT, c + 1)
                plain(pe)
                for t in range(TT):
                    last = pe.transpose(pT[1][:, t * SSM:(t + 1) * SSM], ssT[:, t * P:(t + 1) * P],
                                        ident[0:SSM, 0:SSM])
                last.then_inc(s_ssN, 1)
                pe.wait_ge(s_ssn, (c + 1) * 3)
                plain(pe)
                for t in range(TT):
                    last = pe.transpose(pT[0][0:R + N, t * P:(t + 1) * P], ssn[:, t, 0:R + N], ident[:])
                last.then_inc(s_dtT, 1)
                pe.wait_ge(s_dtB, c + 1)
                for j in range(DT):
                    if j >= 2:
                        pe.wait_ge(s_abs, per_chunk(c, DT, j - 2))
                        pe.wait_ge(s_relu, per_chunk(c, DT, j - 2))
                    pe.matmul(pA[j % 2][:], wdt[:, j * P:(j + 1) * P], dtB[0:R, :],
                              start=True, stop=True).then_inc(s_z, 1)
                pe.wait_ge(s_xlo, (c + 1) * HT)
                plain(pe)

                def turn_h(n, g):
                    pe.wait_ge(s_scan, per_n(c, n, DT, g * GQ + GQ - 1) + SCAN0)
                    for t in range(TT):
                        i = g * TT + t
                        pe.wait_ge(s_stt, per_n(c, n, G * TT, i - 2) + STT0)
                        for q in range(GQ):
                            last = pe.transpose(pT[i % 2][:, q * P:(q + 1) * P],
                                                h[:, g, q, t * P:(t + 1) * P], ident[:])
                        last.then_inc(s_hT, 1)

                def up(n, s, w):
                    pe.wait_ge(s_gu[w], (c * (S * K) + n + 1) * 16)
                    pe.wait_ge(s_hf, unit(c, n, w) - W + FFN0)
                    for part in range(2):
                        for k in range(HT):
                            for xx in (xhi, xlo):
                                last = pe.matmul(pG[w][:, part * ST:(part + 1) * ST], wgu[:, w, part, k],
                                                 xx[:, k, ds(s * ST, ST)], start=(k == 0 and xx is xhi),
                                                 stop=(k == HT - 1 and xx is xlo))
                    last.then_inc(s_up, 1)

                def down(n, k, w, first, last_):
                    pe.wait_ge(s_hlo, unit(c, n, w))
                    for t in range(SB):
                        for hh in (hhi, hlo):
                            last = pe.matmul(pO[t][:], hh[:, w, t * P:(t + 1) * P],
                                             wdn[:, ds(k * W + w, 1)].squeeze(1),
                                             start=(first and w == 0 and hh is hhi),
                                             stop=(last_ and w == W - 1 and hh is hlo))
                    last.then_inc(s_down, 1)

                def step(n, s, k, first, last):
                    if s is not None:
                        for w in range(W):
                            up(n, s, w)
                    for g in range(G):
                        turn_h(n, g)
                    if s is not None:
                        if first:
                            pe.wait_ge(s_ffn, c * (S * SB) + s * SB + ONE)
                        for w in range(W):
                            down(n, k, w, first, last)
                scan_loops(step, None, pe)

                def turn_y(j):
                    if j >= 2:
                        pe.wait_ge(s_y1, per_chunk(c, DT, j - 2))
                    for t in range(TT):
                        last = pe.transpose(pT[j % 2][:, t * P:(t + 1) * P], yT[:, t, j * P:(j + 1) * P], ident[:])
                    last.then_inc(s_yT, 1)

                def project(j):
                    pe.wait_ge(s_wo[j % 2], per_chunk(c, DT // 2, j // 2) * 16)
                    pe.wait_ge(s_y2, per_chunk(c, DT, j))
                    for t in range(TT):
                        last = pe.matmul((pO + pA)[t][:], y2[j % 2][:, t * P:(t + 1) * P], wout[:, j % 2],
                                         start=(j == 0), stop=(j == DT - 1))
                    last.then_inc(s_wout, 1)

                pe.wait_ge(s_stt, per_n(c, N - 1, DT, DT - 1) + STT0)
                pe.wait_ge(s_ffn, (c + 1) * (S * SB) + ONE)
                for j in range(DT):
                    turn_y(j)
                    if j >= 1:
                        project(j - 1)
                project(DT - 1)
            chunk_loops(pe, chunk)


def kernel(**inputs):
    import numpy as np
    import concourse.bacc as bacc
    from concourse.bass_utils import run_bass_kernel_spmd as run

    a = {k.replace("L0_", ""): np.asarray(v) for k, v in inputs.items()}

    def tiles(w, n):
        return w.reshape(n, P, -1).transpose(1, 0, 2)

    w_in = a["attn_W_in"].reshape(2, DT, P, HT, P).transpose(1, 4, 0, 3, 2)
    w_gu = np.stack([a["ffn_W_gate"], a["ffn_W_up"]]).reshape(2, MT, P, HT, P).transpose(1, 4, 0, 3, 2)
    arrays = {
        "x": a["attn_hidden_states"].reshape(CHUNKS, TT, P, H).transpose(0, 2, 1, 3),
        "w_in": w_in,
        "conv_w": tiles(a["attn_conv_w"], DT),
        "conv_b": a["attn_conv_b"].reshape(DT, P).T,
        "w_x": tiles(a["attn_Wx"].T, DT),
        "dt_ln": a["attn_dt_ln_w"], "b_ln": a["attn_b_ln_w"], "c_ln": a["attn_c_ln_w"],
        "w_dt": a["attn_Wdt"].T,
        "dt_bias": a["attn_dt_bias"].reshape(DT, P).T,
        "a_mat": tiles(a["attn_A"], DT),
        "d_par": a["attn_D_param"].reshape(DT, P).T,
        "w_out": a["attn_W_out"].T.reshape(DT, P, H),
        "w_gu": w_gu,
        "w_dn": tiles(a["ffn_W_down"].T, MT).reshape(P, MT * H),
    }
    arrays = {k: np.ascontiguousarray(v) for k, v in arrays.items()}
    nc = bacc.Bacc("TRN2", target_bir_lowering=False, num_devices=1)
    aps = {k: nc.dram_tensor(k, v.shape, mybir.dt.from_np(v.dtype), kind="ExternalInput").ap()
           for k, v in arrays.items()}
    aps["b_rows"] = nc.dram_tensor("b_rows", (CHUNKS, N, T), F32, kind="Internal").ap()
    aps["out"] = nc.dram_tensor("out", (CHUNKS, P, TT, H), F32, kind="ExternalOutput").ap()
    build(nc, **aps)
    got = run(nc, [arrays], core_ids=[0]).results[0]["out"]
    return got.transpose(0, 2, 1, 3).reshape(BATCH, SEQ, H)
```

```python
from contextlib import ExitStack

import concourse.bass as bass
from concourse import mybir

F32 = mybir.dt.float32
F32R = mybir.dt.float32r
F16 = mybir.dt.float16
ALU = mybir.AluOpType
ACT = mybir.ActivationFunctionType
AX = mybir.AxisListType

P = 128
BATCH, SEQ, H = 2, 1024, 512
D, N, TAPS, R = 1024, 16, 4, 32
M = 1792
T = 512
HALVES = SEQ // T
CHUNKS = BATCH * HALVES
TT = T // P
HT = H // P
DT = D // P
MT = M // P
G = 2
Q = DT // G
ST = T // G
SB = ST // P
LN_EPS, RMS_EPS = 1e-5, 1e-6
SSM = R + 2 * N
UP = T + TAPS - 1
DTR = 3 * R

JOBS = (
    {0: [("GT", 0, 0, 3)], 1: [("YT", i, i, i) for i in range(4)], 2: [("WO", 0, 0, 3)], 3: [("GT", 1, 0, 3)],
     4: [("WO", 1, 0, 2), ("Z", 0, 3, 3)], 5: [("GT", 2, 0, 2), ("Z", 1, 3, 3)],
     6: [("WO", 2, 0, 2), ("Z", 2, 3, 3)], 7: [("GT", 3, 0, 2), ("Z", 3, 3, 3)],
     8: [("WO", 3, 0, 3)], 9: [("GT", 4, 0, 3)], 10: [("GT", 5, 0, 2), ("UD", 0, 3, 3)],
     11: [("GT", 6, 0, 2), ("UD", 1, 3, 3)], 12: [("GT", 7, 0, 2), ("UD", 2, 3, 3)], 13: [("UD", 3, 0, 0)],
     14: [("XT", i, i, i) for i in range(4)]},
    {0: [("UT", 0, 0, 3)], **{1 + j: [("UT", 1 + j, 0, 2), ("YT", j, 3, 3)] for j in range(4)},
     5: [("UT", 5, 0, 3)], 6: [("UT", 6, 0, 3)], 7: [("UT", 7, 0, 3)], 8: [("WO", 0, 0, 3)], 9: [("WO", 1, 0, 3)],
     10: [("SSM", 0, 0, 3)], 11: [("WO", 2, 0, 2), ("UD", 0, 3, 3)],
     12: [("DTT", 0, 0, 0), ("Z", 0, 1, 1), ("Z", 1, 2, 2), ("Z", 2, 3, 3)],
     13: [("Z", 3, 0, 0), ("UD", 1, 1, 1), ("UD", 2, 2, 2)], 14: [("WO", 3, 0, 2), ("UD", 3, 3, 3)]},
)
ORDER = tuple([(kind, i) for n in range(N) for kind, i, _, _ in jobs.get(n, [])] for jobs in JOBS)
STEP_OF = tuple({(kind, i): n for n in range(N) for kind, i, _, _ in jobs.get(n, [])} for jobs in JOBS)
QUARTER_OF = tuple({(kind, i): n * Q + q for n in range(N) for kind, i, q, _ in jobs.get(n, [])} for jobs in JOBS)
SOFT_STEP = (8, 13)
NORM_STEP = 9


def build(nc, x, w_in, conv_w, conv_b, w_x, dt_ln, b_ln, c_ln, w_dt, dt_bias, a_mat, d_par, w_out, w_gu, w_dn,
          b_rows, wdn_rows, out):
    with ExitStack() as ctx:
        def sb(name, shape, dt=F32):
            return ctx.enter_context(nc.sbuf_tensor(name, shape, dt))

        def bank(name):
            return ctx.enter_context(nc.psum_tensor(name, [P, 512], F32))

        def sem(name):
            return ctx.enter_context(nc.semaphore(name))

        wx = sb("wx", [P, DT, SSM])
        wdt = sb("wdt", [DTR, D], F32R)
        cw = sb("cw", [P, DT, TAPS])
        cb = sb("cb", [P, DT])
        dtb = sb("dtb", [P, DT])
        dpar = sb("dpar", [P, DT])
        amat = sb("amat", [P, DT, N])
        lnw = sb("lnw", [P, SSM])
        ident = sb("ident", [P, P])
        minus_half = sb("minus_half", [P, TT * 3])
        win = sb("win", [P, 2, HT, P])
        wgu = sb("wgu", [P, 2, 2, HT, P], F16)
        wdn = sb("wdn", [P, 2, H], F32R)
        wout = sb("wout", [P, Q, H])
        brow = sb("brow", [P, 2, T])
        xin = sb("xin", [P, TT, H])
        acc = sb("acc", [P, TT, H])
        yT = sb("yT", [P, G, TT, Q * P])
        cn = sb("cn", [P, TT, N])
        xnT = sb("xnT", [P, HT, T])
        xhi = sb("xhi", [P, HT, T], F16)
        xlo = sb("xlo", [P, HT, T], F16)
        u = sb("u", [P, DT, T])
        gate = sb("gate", [P, DT, T])
        delta = sb("delta", [P, G, Q, T])
        du = sb("du", [P, G, Q, T])
        h = sb("h", [P, 2, Q, T])
        b = sb("b", [P, 2, Q, T])
        shared = sb("shared", [P, 3 * T + 2 * UP])
        conv = shared[:, 0:3 * T].rearrange("p (s t) -> p s t", t=T)
        upad = shared[:, 3 * T:3 * T + 2 * UP].rearrange("p (s t) -> p s t", t=UP)
        sig = sb("sig", [P, 2, T])
        ud = sb("ud", [P, T])
        state = sb("state", [P, 2, DT, N])
        carry = sb("carry", [P, 2, DT, TAPS - 1])
        stats = sb("stats", [P, TT, 6])
        meanvar = sb("meanvar", [P, TT, 2])
        veps = sb("veps", [P, TT])
        rstd = sb("rstd", [P, TT])
        nmr = sb("nmr", [P, TT])
        ssn = sb("ssn", [P, TT, SSM])
        ms = sb("ms", [P, TT, 3])
        mse = sb("mse", [P, TT, 3])
        rms = sb("rms", [P, TT, 3])
        dtT = sb("dtT", [DTR, T], F32R)
        bT = sb("bT", [DTR + N, T])
        th = sb("th", [P, ST])
        v = sb("v", [P, ST])
        hf = sb("hf", [P, 2, ST])
        hhi = sb("hhi", [P, 2, ST], F32R)
        hlo = sb("hlo", [P, 2, ST], F32R)
        xn = shared[:, 0:TT * H].rearrange("p (t h) -> p t h", h=H)
        ss, sq, sw = (shared[:, i * TT * SSM:(i + 1) * TT * SSM].rearrange("p (t k) -> p t k", k=SSM) for i in range(3))
        dts = shared[:, 3 * TT * SSM:3 * TT * SSM + TT * (DTR + N)].rearrange("p (t k) -> p t k", k=DTR + N)
        wdt_raw, wdt_rounded = (gate[0:DTR, 2 * i:2 * i + 2].rearrange("p s t -> p (s t)") for i in range(2))
        wdn16 = yT[:].rearrange("p g t d -> p (g t d)").bitcast(F16)[:, 0:MT * H]
        HALF = MT // 2 * H
        wdn_stage = [z[:].rearrange("p g q t -> p (g q t)")[:, 0:HALF] for z in (delta, du)]

        pA = [bank(f"pA{i}") for i in range(2)]
        pT = [bank(f"pT{i}") for i in range(2)]
        pG = bank("pG")
        pO = [bank(f"pO{i}") for i in range(SB)]
        pX = bank("pX")

        s_const, s_wdn16, s_x = sem("consts_in"), sem("wdn16_in"), sem("x_in")
        s_win, s_gu, s_wd, s_brow = ([sem(f"{n}{i}") for i in range(2)] for n in ("win_in", "gu_in", "wdn_in", "brow_in"))
        s_wo, s_brows, s_out, s_stored = sem("wout_in"), sem("b_rows_stored"), sem("out_stored"), sem("wdn_stored")
        s_zeroed, s_ident, s_half, s_wdn, s_passed = (sem(n) for n in (
            "zeroed", "ident_done", "half_done", "wdn_rounded", "passed"))
        s_full, s_read = sem("side_bank_full"), sem("side_bank_read")
        s_stats, s_mv, s_veps, s_rstd, s_nmr, s_xn, s_xhi, s_xlo, s_acc = (sem(n) for n in (
            "stats", "meanvar", "veps", "rstd", "minus_mean_rstd", "xn", "x_high", "x_low", "acc_is_x"))
        s_head, s_upad, s_conv, s_tail, s_tanh_side, s_sig, s_silu = (sem(n) for n in (
            "upad_head", "upad_tile", "tap_added", "carry_kept", "side_tanh", "sigmoid", "silu"))
        s_ss, s_ms, s_mse, s_rms, s_sw, s_ssn, s_cn = (sem(n) for n in (
            "ss", "mean_squares", "ms_eps", "rms", "ss_weighted", "ss_normed", "c_kept"))
        s_dts, s_wdt = sem("dt_parts"), sem("w_dt_parts")
        s_relu, s_soft, s_delta, s_du, s_ud = (sem(n) for n in ("z_relu", "soft", "delta", "du", "u_d"))
        s_b, s_keep, s_exp, s_scan, s_hT, s_stt = (sem(n) for n in (
            "b_done", "state_kept", "exp_done", "scan_done", "h_turned", "y_added"))
        s_up, s_tanh, s_v, s_hf, s_hhi, s_hlo, s_down, s_ffn = (sem(n) for n in (
            "up_done", "tanh_done", "v_done", "hf_done", "hhi_done", "hlo_done", "down_done", "ffn_added"))

        RING, ONE, BROW0 = 2, 1, 4
        N_SIDE = (len(ORDER[0]), len(ORDER[1]))

        def job(c, g, kind, i):
            return (c + 1) * sum(N_SIDE) + (N_SIDE[0] if g else 0) + ORDER[g].index((kind, i))

        def filled(k):
            return k + 1

        def emptied(k):
            return k + 1 + ONE

        def of_phase(ph, n, q=0, count=1):
            return ph * (N * count) + n * count + q + 1

        def unit(ph, n):
            return ph * MT + n + 1

        def silu(c, g, j):
            return (c + g) * (2 * DT) + (0 if g else DT) + j

        def phases(eng, phase):
            phase(-1, 0, False, False, False, True)
            phase(-1, 1, False, False, True, False)
            phase(0, 0, True, False, True, True)
            with eng.Fori(0, CHUNKS - 2) as c:
                phase(c, 1, True, True, True, False)
                phase(c + 1, 0, True, True, True, True)
            phase(CHUNKS - 2, 1, True, True, True, False)
            phase(CHUNKS - 1, 0, True, True, True, False)
            phase(CHUNKS - 1, 1, True, True, False, False)
            phase(CHUNKS, 0, False, True, False, False)

        def does(kind, post, work, ahead):
            return post if kind in ("YT", "WO") else ahead if kind == "XT" else work

        def ended(g, n, q, post, work, ahead):
            return [(kind, i) for m in range(N) for kind, i, _, last in JOBS[g].get(m, [])
                    if m * Q + last + 1 == n * Q + q and does(kind, post, work, ahead)]

        def scan_before(c, g):
            return not (isinstance(c, int) and c * G + g < 1)

        def plain(eng):
            eng.sem_inc(s_passed, 1)

        consts = [(wx[:], w_x), (cw[:], conv_w), (cb[:], conv_b), (dtb[:], dt_bias),
                  (dpar[:], d_par), (amat[:], a_mat), (lnw[:, 0:R], dt_ln.partition_broadcast(P)),
                  (lnw[:, R:R + N], b_ln.partition_broadcast(P)), (lnw[:, R + N:SSM], c_ln.partition_broadcast(P))]
        consts += [(wdt_raw[i * R:(i + 1) * R], w_dt) for i in range(3)]
        block = ctx.enter_context(nc.Block())

        @block.sync
        def _(sp):
            sp.dma_start(xin[:], x[0]).then_inc(s_x, 16)
            sp.dma_start(win[:, 0], w_in[0, 0]).then_inc(s_win[0], 16)
            for tile, dram in consts:
                sp.dma_start(tile, dram).then_inc(s_const, 16)
            sp.dma_start(wdn16, w_dn).then_inc(s_wdn16, 16)
            sp.sem_inc(s_out, 16)

            def load_win(c, g, j):
                k = silu(c, g, j)
                part = 0 if g else 1
                if not (isinstance(k, int) and k < 2):
                    before = (c, g, j - 2) if j >= 2 else (c, 0, j + DT - 2) if g else (c - 1, 1, j + DT - 2)
                    kind = "UT" if before[1] else "GT"
                    sp.wait_ge(s_full, filled(job(*before[:2], kind, before[2])))
                sp.dma_start(win[:, j % 2], w_in[j, part]).then_inc(s_win[j % 2], 16)

            def load_brow(c, g, n):
                ph = c * G + g
                sp.wait_ge(s_b, of_phase(ph, n - 2, 1, 2) + BROW0)
                sp.dma_start(brow[:, n % 2], b_rows[c, n].partition_broadcast(P)).then_inc(s_brow[n % 2], 16)

            def load_up(ph, n):
                sp.wait_ge(s_up, unit(ph, n - 2) + RING)
                sp.dma_start(wgu[:, n % 2], w_gu[n]).then_inc(s_gu[n % 2], 16)

            def load_down(ph, n):
                sp.wait_ge(s_down, unit(ph, n - 2) + RING)
                sp.dma_start(wdn[:, n % 2].bitcast(F32), wdn_rows[n]).then_inc(s_wd[n % 2], 16)

            def phase(c, g, scan, post, work, ahead):
                ph = c * G + g
                tiles = {STEP_OF[g][("UT" if g else "GT", j)]: j for j in range(DT)} if work else {}
                for n in range(-1, N):
                    if n == -1 and scan:
                        load_up(ph, 0)
                    if n == -1 and scan and ahead:
                        sp.wait_ge(s_xn, (c + 1) * TT)
                        plain(sp)
                        sp.dma_start(xin[:], x[c + 1]).then_inc(s_x, 16)
                    if n == -1 and post:
                        if not (isinstance(c, int) and (c, g) == (0, 1)):
                            sp.wait_ge(s_full, filled(job(c, 0, "WO", Q - 1) if g else job(c - 1, 1, "WO", Q - 1)))
                        first = 0 if g else Q
                        sp.dma_start(wout[:], w_out[:, first:first + Q]).then_inc(s_wo, 16)
                    if scan and n + 1 < N and n >= 0:
                        load_brow(c, g, n + 1)
                    if scan and 0 <= n and n + 1 < MT:
                        load_up(ph, n + 1)
                    if n >= 0 and n + 1 in tiles:
                        load_win(c, g, tiles[n + 1])
                    if scan and 0 <= n - 1 < MT:
                        if n == 1 and isinstance(ph, int) and ph == 0:
                            sp.wait_ge(s_stored, 32)
                        load_down(ph, n - 1)
                    if n == 4 and isinstance(c, int) and (c, g) == (-1, 1):
                        sp.wait_ge(s_wdn, 2)
                        for i in range(2):
                            sp.dma_start(wdn_rows[i * (MT // 2):(i + 1) * (MT // 2)].rearrange("m p h -> p m h"),
                                         wdn_stage[i].rearrange("p (m h) -> p m h", h=H)).then_inc(s_stored, 16)
                    if n == STEP_OF[1][("DTT", 0)] + 1 and g == 1 and work:
                        sp.wait_ge(s_read, emptied(job(c, 1, "DTT", 0)))
                        sp.dma_start(b_rows[c + 1], bT[DTR:DTR + N]).then_inc(s_brows, 16)
                    if n == N - 1 and work:
                        if g == 1:
                            sp.wait_ge(s_brows, (c + 2) * 16)
                            plain(sp)
                        load_brow(*((c + 1, 0) if g else (c, 1)), 0)
                    if n == N - 1 and g == 0 and ahead and not (isinstance(c, int) and c < 0):
                        load_win(c, 1, 0)
                    if n == N - 1 and g == 1 and work:
                        load_win(c + 1, 0, 0)
                    if post and g == 0 and n == STEP_OF[0][("WO", Q - 1)] + 2:
                        sp.wait_ge(s_read, emptied(job(c, 0, "WO", Q - 1)))
                        sp.dma_start(out[c - 1], acc[:]).then_inc(s_out, 16)
                    if scan and g == 0 and n == STEP_OF[0][("WO", Q - 1)] + 4:
                        sp.wait_ge(s_out, (c + 1) * 16)
                        plain(sp)
                        sp.dma_start(acc[:], x[c]).then_inc(s_acc, 16)
                plain(sp)
            phases(sp, phase)
            sp.wait_ge(s_out, (CHUNKS + 1) * 16)

        @block.gpsimd
        def _(pool):
            pool.sem_inc(s_b, BROW0)
            pool.sem_inc(s_keep, RING)
            pool.sem_inc(s_silu, RING)
            pool.sem_inc(s_hlo, RING)
            pool.memset(ident[:], 0.0).then_inc(s_zeroed, 1)
            pool.memset(state[:], 0.0).then_inc(s_zeroed, 1)
            pool.memset(carry[:], 0.0).then_inc(s_zeroed, 1)
            pool.memset(minus_half[:], -0.5).then_inc(s_half, 1)
            pool.wait_ge(s_zeroed, 3)
            pool.affine_select(out=ident[:], in_=ident[:], compare_op=ALU.not_equal, fill=1.0, base=0,
                               pattern=[[-1, P]], channel_multiplier=1).then_inc(s_ident, 1)
            pool.wait_ge(s_half, 1)

            def make_b(c, g, n, half):
                ph = c * G + g
                if half == 0:
                    pool.wait_ge(s_brow[n % 2], (ph * (N // 2) + n // 2 + 1) * 16)
                qs = slice(half * (Q // 2), (half + 1) * (Q // 2))
                pool.tensor_tensor(b[:, n % 2, qs], du[:, g, qs], brow[:, n % 2].unsqueeze(1).broadcast_to([P, Q // 2, T]),
                                   ALU.mult).then_inc(s_b, 1)

            def keep_state(ph, g, n):
                pool.wait_ge(s_scan, of_phase(ph, n, Q - 1, Q) + RING)
                plain(pool)
                pool.tensor_copy(state[:, 1, g * Q:(g + 1) * Q, n:n + 1], h[:, n % 2, :, T - 1:T]).then_inc(s_keep, 1)

            def phase(c, g, scan, post, work, ahead):
                ph = c * G + g
                cc = c + 1

                def between(n):
                    if g == 1 and work:
                        j = n - STEP_OF[1][("UT", 0)]
                        if 0 < j <= DT:
                            pool.wait_ge(s_head, cc * DT + j)
                            pool.wait_ge(s_upad, cc * DT + j)
                            plain(pool)
                            pool.tensor_copy(carry[:, 1, j - 1], upad[:, (j - 1) % 2, T:UP]).then_inc(s_tail, 1)
                        if 0 <= j < DT:
                            if j == 0:
                                pool.wait_ge(s_full, filled(job(c, 0, "XT", HT - 1)))
                            if j >= 2:
                                pool.wait_ge(s_conv, (cc * DT + j - 1) * (TAPS - 1))
                            plain(pool)
                            pool.tensor_copy(upad[:, j % 2, 0:TAPS - 1], carry[:, cc % 2, j]).then_inc(s_head, 1)
                        if n == STEP_OF[1][("SSM", 0)] + 1:
                            pool.wait_ge(s_mse, (cc + 1) * 2)
                            pool.tensor_tensor(rms[:].rearrange("p t k -> p (t k)"),
                                               mse[:].rearrange("p t k -> p (t k)"), minus_half[:],
                                               ALU.pow).then_inc(s_rms, 1)
                        if 0 <= j - 2 < DT:
                            k = silu(c, 1, j - 2)
                            pool.wait_ge(s_sig, k + 1)
                            pool.tensor_tensor(u[:, j - 2], conv[:, (j - 2) % 3], sig[:, (j - 2) % 2], ALU.mult).then_inc(s_silu, 1)
                    if g == 0 and work:
                        for j in range(DT):
                            if STEP_OF[0][("GT", j)] == n - 1:
                                k = silu(c, 0, j)
                                pool.wait_ge(s_sig, k + 1)
                                pool.tensor_tensor(gate[:, j], gate[:, j], sig[:, j % 2], ALU.mult).then_inc(s_silu, 1)

                if scan_before(c, g):
                    keep_state(ph - 1, 1 - g, N - 1)
                for n in range(N):
                    if ahead and n == NORM_STEP:
                        pool.wait_ge(s_veps, cc + 1)
                        pool.tensor_tensor(rstd[:], veps[:], minus_half[:, 0:TT], ALU.pow).then_inc(s_rstd, 1)
                    if scan and n >= 1:
                        keep_state(ph, g, n - 1)
                    for half in range(2):
                        if half == 1:
                            between(n)
                        if n + 1 < N and scan:
                            make_b(c, g, n + 1, half)
                        if n + 1 == N and work:
                            if half == 0:
                                pool.wait_ge(s_du, (ph + 2) * 2)
                            make_b(*((c + 1, 0) if g else (c, 1)), 0, half)
                    if work and g == 0 and 0 <= n - SOFT_STEP[0] - 1 < 4:
                        i = n - SOFT_STEP[0] - 1
                        qs = slice(i % 2 * (Q // 2), (i % 2 + 1) * (Q // 2))
                        if i < 2:
                            pool.wait_ge(s_soft, (ph + 1) * 2 + 2)
                            pool.tensor_tensor(delta[:, 1, qs], delta[:, 1, qs], du[:, 1, qs], ALU.add).then_inc(s_delta, 1)
                        else:
                            pool.wait_ge(s_delta, (ph + 1) * 2 + i - 1)
                            pool.tensor_tensor(du[:, 1, qs], delta[:, 1, qs], u[:, Q + i % 2 * (Q // 2):Q + (i % 2 + 1) * (Q // 2)],
                                               ALU.mult).then_inc(s_du, 1)
                    if scan and 1 <= n <= MT:
                        pool.wait_ge(s_hhi, unit(ph, n - 1))
                        pool.wait_ge(s_down, unit(ph, n - 3) + RING)
                        pool.tensor_tensor(hlo[:, (n - 1) % 2], hf[:, (n - 1) % 2], hhi[:, (n - 1) % 2].bitcast(F32),
                                           ALU.subtract).then_inc(s_hlo, 1)
                plain(pool)
            phases(pool, phase)

        @block.scalar
        def _(act):
            def phase(c, g, scan, post, work, ahead):
                ph = c * G + g
                cc = c + 1
                nph, ng = ph + 1, 1 - g

                def empty(kind, i):
                    k = job(c, g, kind, i)
                    act.wait_ge(s_full, filled(k))
                    if kind == "XT":
                        act.copy(xnT[:, i], pX[:]).then_inc(s_read, 1)
                    elif kind == "UT":
                        if i >= 2:
                            act.wait_ge(s_tail, cc * DT + i - 1)
                            act.wait_ge(s_conv, (cc * DT + i - 1) * (TAPS - 1))
                        if i >= 3:
                            act.wait_ge(s_silu, silu(c, 1, i - 3) + 1 + RING)
                        act.copy(upad[:, i % 2, TAPS - 1:UP], pX[:]).then_inc(s_read, 1)
                        act.wait_ge(s_read, emptied(k))
                        act.activation(conv[:, i % 3], upad[:, i % 2, TAPS - 1:UP], ACT.Identity, bias=cb[:, i:i + 1],
                                       scale=cw[:, i, TAPS - 1:TAPS]).then_inc(s_upad, 1)
                    elif kind == "GT":
                        act.copy(gate[:, i], pX[:]).then_inc(s_read, 1)
                        act.wait_ge(s_silu, silu(c, 0, i) - 2 + 1 + RING)
                        act.wait_ge(s_read, emptied(k))
                        act.activation(sig[:, i % 2], gate[:, i], ACT.Tanh, scale=0.5).then_inc(s_tanh_side, 1)
                        act.wait_ge(s_tanh_side, silu(c, 0, i) + 1)
                        act.activation(sig[:, i % 2], sig[:, i % 2], ACT.Copy, scale=0.5, bias=0.5).then_inc(s_sig, 1)
                    elif kind == "SSM":
                        act.copy(shared[:, 0:TT * SSM], pX[:, 0:TT * SSM]).then_inc(s_ss, 1)
                        act.activation(shared[:, TT * SSM:2 * TT * SSM], pX[:, 0:TT * SSM],
                                       ACT.Square).then_inc(s_read, 1)
                    elif kind == "DTT":
                        act.copy(dtT[:], pX[0:DTR, :])
                        act.copy(bT[DTR:DTR + N], pX[DTR:DTR + N, :]).then_inc(s_read, 1)
                    elif kind == "Z":
                        act.activation(du[:, ng, i], pX[:], ACT.Relu,
                                       bias=dtb[:, ng * Q + i:ng * Q + i + 1]).then_inc(s_relu, 1)
                        act.activation(delta[:, ng, i], pX[:], ACT.Abs,
                                       bias=dtb[:, ng * Q + i:ng * Q + i + 1]).then_inc(s_read, 1)
                    elif kind == "UD":
                        act.copy(yT[:, ng, :, i * P:(i + 1) * P],
                                 pX[:].rearrange("p (t d) -> p t d", d=P)).then_inc(s_read, 1)

                def decay(p, pg, n, q):
                    act.wait_ge(s_scan, of_phase(p, n, q - 2, Q) + RING)
                    j = pg * Q + q
                    act.activation(pA[q % 2][:], delta[:, pg, q], ACT.Exp, scale=amat[:, j, n:n + 1]).then_inc(s_exp, 1)

                def scale_u(i):
                    j = ng * Q + i
                    act.wait_ge(s_silu, (silu(c, 1, j) if g else silu(c - 1, 1, j)) + 1 + RING)
                    if i:
                        act.wait_ge(s_full, filled(job(c, g, "UD", i - 1)))
                    act.activation(ud[:], u[:, j], ACT.Copy, scale=dpar[:, j:j + 1]).then_inc(s_ud, 1)

                for n in range(N):
                    if isinstance(c, int) and (c, g) == (-1, 1) and n == 0:
                        act.wait_ge(s_const, 16 * len(consts))
                    if isinstance(c, int) and (c, g) == (-1, 1) and n == STEP_OF[1][("SSM", 0)]:
                        act.wait_ge(s_stored, 32)
                    for q in range(Q):
                        if scan and (n, q) != (N - 1, Q - 1):
                            decay(ph, g, n + (q + 1) // Q, (q + 1) % Q)
                        if work and (n, q) == (N - 1, Q - 1):
                            act.wait_ge(s_delta, (nph + 1) * 2)
                            decay(nph, ng, 0, 0)
                        if scan and q == 3 and n < MT:
                            act.wait_ge(s_up, unit(ph, n) + RING)
                            act.activation(th[:], pG[:, 0:ST], ACT.Tanh, scale=0.5).then_inc(s_tanh, 1)
                        for kind, i in ended(g, n, q, post, work, ahead):
                            if kind not in ("YT", "WO"):
                                empty(kind, i)
                        if scan and q == 1 and 1 <= n <= MT:
                            act.wait_ge(s_hf, unit(ph, n - 1) + ONE)
                            act.wait_ge(s_down, unit(ph, n - 3) + RING)
                            act.copy(hhi[:, (n - 1) % 2], hf[:, (n - 1) % 2]).then_inc(s_hhi, 1)
                        if ahead and n == NORM_STEP + 1:
                            act.wait_ge(s_nmr, cc + 1)
                            act.activation(xn[:, q], xin[:, q], ACT.Identity, bias=nmr[:, q:q + 1],
                                           scale=rstd[:, q:q + 1]).then_inc(s_xn, 1)
                        if g == 1 and work and q < 2:
                            j = n - 2 - STEP_OF[1][("UT", 0)]
                            k = silu(c, 1, j)
                            if 0 <= j < DT and q == 0:
                                act.wait_ge(s_conv, (cc * DT + j + 1) * (TAPS - 1))
                                act.wait_ge(s_silu, k - 2 + 1 + RING)
                                act.activation(sig[:, j % 2], conv[:, j % 3], ACT.Tanh, scale=0.5).then_inc(s_tanh_side, 1)
                            if 0 <= j < DT and q == 1:
                                act.wait_ge(s_tanh_side, k + 1)
                                act.activation(sig[:, j % 2], sig[:, j % 2], ACT.Copy, scale=0.5, bias=0.5).then_inc(s_sig, 1)
                        if work and (n, q) == (SOFT_STEP[g], 1):
                            act.wait_ge(s_read, emptied(job(c, g, "Z", Q - 1)))
                            act.activation(delta[:, ng], delta[:, ng], ACT.Exp, scale=-1.0).then_inc(s_soft, 1)
                        if work and (n, q) == (SOFT_STEP[g], 3):
                            act.wait_ge(s_soft, nph * 2 + 1)
                            act.activation(delta[:, ng], delta[:, ng], ACT.Ln, bias=1.0).then_inc(s_soft, 1)
                        if g == 1 and work and n == N - 2 and q == 3:
                            if scan:
                                act.wait_ge(s_up, unit(ph, MT - 1) + RING)
                            act.copy(xhi[:], xnT[:]).then_inc(s_xhi, 1)
                        for i in range(Q):
                            if work and n * Q + q + 1 == QUARTER_OF[g][("UD", i)]:
                                scale_u(i)
                plain(act)
            phases(act, phase)

        @block.vector
        def _(dve):
            for s, start in ((s_scan, RING), (s_stt, RING), (s_hf, ONE), (s_ffn, ONE), (s_read, ONE)):
                dve.sem_inc(s, start)

            def prepare():
                dve.wait_ge(s_const, 16 * len(consts))
                dve.tensor_copy(wdt_rounded[2 * R:DTR].bitcast(F32R), wdt_raw[2 * R:DTR]).then_inc(s_wdt, 1)
                dve.tensor_copy(wdt[0:2 * R], wdt_raw[0:2 * R]).then_inc(s_wdt, 1)
                dve.wait_ge(s_wdt, 2)
                dve.tensor_tensor(wdt[2 * R:DTR], wdt_raw[2 * R:DTR], wdt_rounded[2 * R:DTR], ALU.subtract).then_inc(s_wdt, 1)
                dve.wait_ge(s_wdn16, 16)
                for i in range(2):
                    dve.tensor_copy(wdn_stage[i], wdn16[:, i * HALF:(i + 1) * HALF]).then_inc(s_wdn, 1)

            def phase(c, g, scan, post, work, ahead):
                ph = c * G + g
                cc = c + 1
                nph, ng = ph + 1, 1 - g

                def add_y(p, pg, n, t):
                    dve.wait_ge(s_hT, of_phase(p, n, t, TT))
                    dve.scalar_tensor_tensor(yT[:, pg, t], pT[t % 2][:], cn[:, t, n:n + 1], yT[:, pg, t],
                                             ALU.mult, ALU.add).then_inc(s_stt, 1)

                def empty(kind, i):
                    k = job(c, g, kind, i)
                    if kind == "YT":
                        j = ng * Q + i
                        dve.wait_ge(s_full, filled(k))
                        dve.wait_ge(s_silu, (silu(c, 0, j) if g else silu(c - 1, 0, j)) + 1 + RING)
                        dve.tensor_tensor(gate[:, j], pX[:], gate[:, j], ALU.mult).then_inc(s_read, 1)
                    elif kind == "WO":
                        dve.wait_ge(s_full, filled(k))
                        if i == 0:
                            dve.wait_ge(s_ffn, ph * SB + ONE)
                        dve.tensor_tensor(acc[:, i], acc[:, i], pX[:], ALU.add).then_inc(s_read, 1)

                def rms_sums():
                    parts = [(0, R), (R, R + N), (R + N, SSM)]
                    dve.wait_ge(s_ss, cc + 1)
                    dve.wait_ge(s_read, emptied(job(c, g, "SSM", 0)))
                    for i, (lo, hi) in enumerate(parts):
                        dve.tensor_reduce(ms[:, :, i:i + 1], sq[:, :, lo:hi], AX.X, ALU.add).then_inc(s_ms, 1)
                    dve.tensor_tensor(sw[:], ss[:], lnw[:].unsqueeze(1).broadcast_to([P, TT, SSM]),
                                      ALU.mult).then_inc(s_sw, 1)
                    dve.wait_ge(s_ms, (cc + 1) * 3)
                    dve.tensor_scalar(mse[:, :, 0:1], ms[:, :, 0:1], 1.0 / R, RMS_EPS, ALU.mult, ALU.add).then_inc(s_mse, 1)
                    dve.tensor_scalar(mse[:, :, 1:3], ms[:, :, 1:3], 1.0 / N, RMS_EPS, ALU.mult, ALU.add).then_inc(s_mse, 1)

                def rms_norms():
                    parts = [(0, R), (R, R + N), (R + N, SSM)]
                    dve.wait_ge(s_rms, cc + 1)
                    dve.wait_ge(s_sw, cc + 1)
                    for i, (lo, hi) in enumerate(parts):
                        to = dts[:, :, DTR:DTR + N] if i == 1 else ssn[:, :, lo:hi]
                        dve.tensor_tensor(to, sw[:, :, lo:hi],
                                          rms[:, :, i:i + 1].broadcast_to([P, TT, hi - lo]), ALU.mult).then_inc(s_ssn, 1)
                    dve.wait_ge(s_ssn, cc * 3 + 1)
                    dve.tensor_copy(dts[:, :, 0:R].bitcast(F32R), ssn[:, :, 0:R]).then_inc(s_dts, 1)
                    dve.tensor_copy(dts[:, :, 2 * R:DTR].bitcast(F32R), ssn[:, :, 0:R]).then_inc(s_dts, 1)
                    dve.wait_ge(s_dts, cc * 3 + 1)
                    dve.tensor_tensor(dts[:, :, R:2 * R], ssn[:, :, 0:R], dts[:, :, 0:R], ALU.subtract).then_inc(s_dts, 1)

                if isinstance(c, int) and (c, g) == (-1, 1):
                    prepare()
                for n in range(N):
                    if ahead and n == NORM_STEP:
                        dve.wait_ge(s_x, (cc + 1) * 16)
                        for t in range(TT):
                            dve.bn_stats(stats[:, t], xin[:, t]).then_inc(s_stats, 1)
                        for t in range(TT):
                            dve.wait_ge(s_stats, cc * TT + t + 1)
                            plain(dve)
                            dve.bn_aggr(meanvar[:, t], stats[:, t]).then_inc(s_mv, 1)
                        dve.wait_ge(s_mv, (cc + 1) * TT)
                        dve.tensor_scalar(veps[:], meanvar[:, :, 1], LN_EPS, None, ALU.add).then_inc(s_veps, 1)
                    for q in range(Q):
                        if scan:
                            if q == 0:
                                dve.wait_ge(s_keep, of_phase(ph, n - 2) + RING)
                            if q % 2 == 0:
                                dve.wait_ge(s_b, of_phase(ph, n, q // 2, 2) + BROW0)
                            dve.wait_ge(s_exp, of_phase(ph, n, q, Q))
                            j = g * Q + q
                            dve.tensor_tensor_scan(h[:, n % 2, q], pA[q % 2][:], b[:, n % 2, q],
                                                   state[:, c % HALVES, j, n:n + 1], ALU.mult, ALU.add).then_inc(s_scan, 1)
                        for kind, i in ended(g, n, q, post, work, ahead):
                            empty(kind, i)
                        if scan and 1 <= n <= MT and q == 0:
                            dve.wait_ge(s_tanh, unit(ph, n - 1))
                            dve.scalar_tensor_tensor(v[:], th[:], 1.0, pG[:, ST:2 * ST], ALU.add, ALU.mult).then_inc(s_v, 1)
                        if n == 0 and scan_before(c, g):
                            add_y(ph - 1, 1 - g, N - 1, q)
                        if n >= 1 and scan:
                            if n == 1 and q == 0:
                                dve.wait_ge(s_cn, c + 1)
                                dve.wait_ge(s_read, emptied(job(c - 1, 1, "UD", Q - 1) if g == 0 else job(c, 0, "UD", Q - 1)))
                            add_y(ph, g, n - 1, q)
                        if scan and 1 <= n <= MT and q == 0:
                            dve.wait_ge(s_v, unit(ph, n - 1))
                            dve.wait_ge(s_hlo, unit(ph, n - 3) + RING)
                            dve.scalar_tensor_tensor(hf[:, (n - 1) % 2], pG[:, 0:ST], 0.5, v[:],
                                                     ALU.mult, ALU.mult).then_inc(s_hf, 1)
                        if ahead and n == NORM_STEP and q == 3:
                            dve.wait_ge(s_rstd, cc + 1)
                            dve.scalar_tensor_tensor(nmr[:], meanvar[:, :, 0], -1.0, rstd[:], ALU.mult, ALU.mult).then_inc(s_nmr, 1)
                        if g == 1 and work:
                            j = n - 1 - STEP_OF[1][("UT", 0)]
                            if 0 <= j < DT and q >= 1:
                                if q == 1:
                                    dve.wait_ge(s_head, cc * DT + j + 1)
                                    dve.wait_ge(s_upad, cc * DT + j + 1)
                                else:
                                    dve.wait_ge(s_conv, (cc * DT + j) * (TAPS - 1) + q - 1)
                                dve.scalar_tensor_tensor(conv[:, j % 3], upad[:, j % 2, q - 1:q - 1 + T], cw[:, j, q - 1:q],
                                                         conv[:, j % 3], ALU.mult, ALU.add).then_inc(s_conv, 1)
                            if n == STEP_OF[1][("SSM", 0)] + 1 and q == 1:
                                rms_sums()
                            if n == STEP_OF[1][("SSM", 0)] + 1 and q == 3:
                                rms_norms()
                            if n == N - 1 and q == 0:
                                dve.wait_ge(s_xhi, cc + 1)
                                dve.tensor_tensor(xlo[:], xnT[:], xhi[:], ALU.subtract).then_inc(s_xlo, 1)
                        if work and g == 1 and (n, q) == (SOFT_STEP[1] + 1, 1):
                            dve.wait_ge(s_soft, nph * 2 + 2)
                            dve.tensor_tensor(delta[:, ng], delta[:, ng], du[:, ng], ALU.add).then_inc(s_delta, 2)
                        if work and g == 1 and (n, q) == (SOFT_STEP[1] + 1, 2):
                            dve.wait_ge(s_delta, (nph + 1) * 2)
                            dve.tensor_tensor(du[:, ng], delta[:, ng], u[:, ng * Q:(ng + 1) * Q], ALU.mult).then_inc(s_du, 2)
                    if scan and g == 0 and n == 0:
                        dve.wait_ge(s_stt, of_phase(ph - 1, N - 1, TT - 1, TT) + RING)
                        dve.wait_ge(s_ssn, (c + 1) * 3)
                        plain(dve)
                        dve.tensor_copy(cn[:], ssn[:, :, R + N:SSM]).then_inc(s_cn, 1)
                if scan:
                    dve.wait_ge(s_down, unit(ph, MT - 1) + RING)
                    dve.wait_ge(s_acc, (c + 1) * 16)
                    if g == 1:
                        dve.wait_ge(s_read, emptied(job(c, 1, "WO", Q - 1)))
                    for t in range(SB):
                        dve.tensor_tensor(acc[:, g * SB + t], acc[:, g * SB + t], pO[t][:], ALU.add).then_inc(s_ffn, 1)
                plain(dve)
            phases(dve, phase)

        @block.tensor
        def _(pe):
            pe.sem_inc(s_up, RING)
            pe.sem_inc(s_down, RING)
            pe.wait_ge(s_ident, 1)

            def phase(c, g, scan, post, work, ahead):
                ph = c * G + g
                cc = c + 1
                ng = 1 - g

                def turn_h(p, n, t):
                    if t == 0:
                        pe.wait_ge(s_scan, of_phase(p, n, Q - 1, Q) + RING)
                    pe.wait_ge(s_stt, of_phase(p, n, t - 2, TT) + RING)
                    for q in range(Q):
                        last = pe.transpose(pT[t % 2][:, q * P:(q + 1) * P], h[:, n % 2, q, t * P:(t + 1) * P], ident[:])
                    last.then_inc(s_hT, 1)

                def up(n, part):
                    if part == 0:
                        pe.wait_ge(s_gu[n % 2], (ph * (MT // 2) + n // 2 + 1) * 16)
                        pe.wait_ge(s_hf, unit(ph, n - 1) + ONE)
                    for k in range(HT):
                        for xx in (xhi, xlo):
                            last = pe.matmul(pG[:, part * ST:(part + 1) * ST], wgu[:, n % 2, part, k],
                                             xx[:, k, g * ST:(g + 1) * ST], start=(k == 0 and xx is xhi),
                                             stop=(k == HT - 1 and xx is xlo))
                    if part == 1:
                        last.then_inc(s_up, 1)

                def down(n):
                    if n == 0:
                        pe.wait_ge(s_ffn, ph * SB + ONE)
                    pe.wait_ge(s_wd[n % 2], (ph * (MT // 2) + n // 2 + 1) * 16)
                    pe.wait_ge(s_hlo, unit(ph, n) + RING)
                    for t in range(SB):
                        for hh in (hhi, hlo):
                            last = pe.matmul(pO[t][:], hh[:, n % 2, t * P:(t + 1) * P], wdn[:, n % 2],
                                             start=(n == 0 and hh is hhi), stop=(n == MT - 1 and hh is hlo))
                    last.then_inc(s_down, 1)

                def side(kind, i, k, part, parts):
                    first, last = part == 0, None
                    if kind in ("UT", "GT"):
                        if first:
                            pe.wait_ge(s_win[i % 2], (silu(c, g, i) // 2 + 1) * 16)
                        for m in range(HT * part // parts, HT * (part + 1) // parts):
                            last = pe.matmul(pX[:], win[:, i % 2, m], xnT[:, m], start=(m == 0), stop=(m == HT - 1))
                    elif kind == "WO":
                        if first and i == 0:
                            pe.wait_ge(s_wo, ph * 16)
                        for m in range(Q * part // parts, Q * (part + 1) // parts):
                            last = pe.matmul(pX[:], gate[:, ng * Q + m, i * P:(i + 1) * P], wout[:, m],
                                             start=(m == 0), stop=(m == Q - 1))
                    elif kind == "SSM":
                        if first:
                            pe.wait_ge(s_silu, silu(c, 1, DT - 1) + 1 + RING)
                        for t in range(TT * part // parts, TT * (part + 1) // parts):
                            for m in range(DT):
                                last = pe.matmul(pX[:, t * SSM:(t + 1) * SSM], u[:, m, t * P:(t + 1) * P], wx[:, m],
                                                 start=(m == 0), stop=(m == DT - 1))
                    elif kind == "Z":
                        j = ng * Q + i
                        last = pe.matmul(pX[:], wdt[:, j * P:(j + 1) * P], dtT[:],
                                         start=True, stop=True)
                    else:
                        if kind == "XT" and i == 0:
                            pe.wait_ge(s_xn, (cc + 1) * TT)
                        if kind == "YT" and i == 0:
                            pe.wait_ge(s_stt, of_phase(ph - 1, N - 1, TT - 1, TT) + RING)
                        if kind == "UD":
                            pe.wait_ge(s_ud, (ph + 1) * Q + i + 1)
                        if kind == "DTT":
                            pe.wait_ge(s_ssn, (cc + 1) * 3)
                            pe.wait_ge(s_dts, (cc + 1) * 3)
                        plain(pe)
                        for t in range(TT):
                            ts = slice(t * P, (t + 1) * P)
                            if kind == "XT":
                                last = pe.transpose(pX[:, ts], xn[:, t, i * P:(i + 1) * P], ident[:])
                            elif kind == "YT":
                                last = pe.transpose(pX[:, ts], yT[:, ng, t, i * P:(i + 1) * P], ident[:])
                            elif kind == "UD":
                                last = pe.transpose(pX[:, ts], ud[:, ts], ident[:])
                            elif kind == "DTT":
                                last = pe.transpose(pX[0:DTR + N, ts], dts[:, t], ident[:])
                    if part == parts - 1:
                        last.then_inc(s_full, 1)

                if isinstance(c, int) and (c, g) == (-1, 1):
                    pe.wait_ge(s_const, 16 * len(consts))
                    pe.wait_ge(s_wdt, 3)
                for n in range(N):
                    for q in range(Q):
                        if n == 0 and scan_before(c, g) and q < 3:
                            turn_h(ph - 1, N - 1, q + 1)
                        if n >= 1 and scan and q < 3:
                            turn_h(ph, n - 1, q + 1)
                        if scan and q == 3:
                            turn_h(ph, n, 0)
                        if scan:
                            if q == 0 and 2 <= n < MT + 2:
                                down(n - 2)
                            if q == 1 and n == 0:
                                pe.wait_ge(s_xlo, c + 1)
                            if 1 <= q <= 2 and n < MT:
                                up(n, q - 1)
                        for kind, i, q0, q1 in JOBS[g].get(n, []):
                            if q0 <= q <= q1:
                                k = job(c, g, kind, i)
                                if q == q0:
                                    pe.wait_ge(s_read, emptied(k - 1))
                                if does(kind, post, work, ahead):
                                    side(kind, i, k, q - q0, q1 - q0 + 1)
                                elif q == q1:
                                    pe.sem_inc(s_full, 1)
                                    pe.sem_inc(s_read, 1)
                plain(pe)
            phases(pe, phase)


def kernel(**inputs):
    import numpy as np
    import concourse.bacc as bacc
    from concourse.bass_utils import run_bass_kernel_spmd as run

    a = {k.replace("L0_", ""): np.asarray(v) for k, v in inputs.items()}

    def tiles(w, n):
        return w.reshape(n, P, -1).transpose(1, 0, 2)

    w_in = a["attn_W_in"].reshape(2, DT, P, HT, P).transpose(1, 0, 4, 3, 2)
    w_gu = np.stack([a["ffn_W_gate"], a["ffn_W_up"]]).reshape(2, MT, P, HT, P).transpose(1, 4, 0, 3, 2)
    arrays = {
        "x": a["attn_hidden_states"].reshape(CHUNKS, TT, P, H).transpose(0, 2, 1, 3),
        "w_in": w_in,
        "conv_w": tiles(a["attn_conv_w"], DT),
        "conv_b": a["attn_conv_b"].reshape(DT, P).T,
        "w_x": tiles(a["attn_Wx"].T, DT),
        "dt_ln": a["attn_dt_ln_w"], "b_ln": a["attn_b_ln_w"], "c_ln": a["attn_c_ln_w"],
        "w_dt": a["attn_Wdt"].T,
        "dt_bias": a["attn_dt_bias"].reshape(DT, P).T,
        "a_mat": tiles(a["attn_A"], DT),
        "d_par": a["attn_D_param"].reshape(DT, P).T,
        "w_out": tiles(a["attn_W_out"].T, DT),
        "w_gu": w_gu,
        "w_dn": tiles(a["ffn_W_down"].T, MT).reshape(P, MT * H),
    }
    arrays = {k: np.ascontiguousarray(v) for k, v in arrays.items()}
    nc = bacc.Bacc("TRN2", target_bir_lowering=False, num_devices=1)
    aps = {k: nc.dram_tensor(k, v.shape, mybir.dt.from_np(v.dtype), kind="ExternalInput").ap()
           for k, v in arrays.items()}
    aps["b_rows"] = nc.dram_tensor("b_rows", (CHUNKS, N, T), F32, kind="Internal").ap()
    aps["wdn_rows"] = nc.dram_tensor("wdn_rows", (MT, P, H), F32, kind="Internal").ap()
    aps["out"] = nc.dram_tensor("out", (CHUNKS, P, TT, H), F32, kind="ExternalOutput").ap()
    build(nc, **aps)
    got = run(nc, [arrays], core_ids=[0]).results[0]["out"]
    return got.transpose(0, 2, 1, 3).reshape(BATCH, SEQ, H)
```

```python
from contextlib import ExitStack

import concourse.bass as bass
from concourse import mybir

F32 = mybir.dt.float32
F32R = mybir.dt.float32r
F16 = mybir.dt.float16
ALU = mybir.AluOpType
ACT = mybir.ActivationFunctionType
AX = mybir.AxisListType

P = 128
BATCH, SEQ, H = 2, 1024, 512
D, N, TAPS, R = 1024, 16, 4, 32
M = 1792
T = 512
HALVES = SEQ // T
CHUNKS = BATCH * HALVES
TT = T // P
HT = H // P
DT = D // P
MT = M // P
G = 2
Q = DT // G
ST = T // G
SB = ST // P
LN_EPS, RMS_EPS = 1e-5, 1e-6
SSM = R + 2 * N
UP = T + TAPS - 1
DTR = 3 * R

JOBS = (
    {0: [("GT", 0, 0, 3)], 1: [("YT", i, i, i) for i in range(4)], 2: [("WO", 0, 0, 3)], 3: [("WO", 1, 0, 3)],
     4: [("WO", 2, 0, 3)], 5: [("WO", 3, 0, 3)], 6: [("Z", i, i, i) for i in range(4)], 7: [("GT", 1, 0, 3)],
     **{8 + i: [("GT", 2 + i, 0, 3)] for i in range(6)},
     **{14 + j: [(kind, 2 * j + i, 2 * m + i, 2 * m + i) for m, kind in enumerate(("UD", "XT")) for i in range(2)]
        for j in range(2)}},
    {**{j: [("UT", j, 0, 3)] for j in range(DT)}, 8: [("SSM", 0, 0, 7)],
     10: [("YT", i, i, i) for i in range(4)], 11: [("DTT", 0, 0, 0), *(("Z", i, i + 1, i + 1) for i in range(3))],
     12: [("Z", 3, 0, 0), ("WO", 0, 1, 3)], 13: [("WO", 1, 0, 2), ("UD", 0, 3, 3)],
     14: [("WO", 2, 0, 2), ("UD", 1, 3, 3)], 15: [("WO", 3, 0, 2), ("UD", 2, 3, 3), ("UD", 3, 3, 3)]},
)
ORDER = tuple([(kind, i) for n in range(N) for kind, i, _, _ in jobs.get(n, [])] for jobs in JOBS)
STEP_OF = tuple({(kind, i): n for n in range(N) for kind, i, _, _ in jobs.get(n, [])} for jobs in JOBS)
QUARTER_OF = tuple({(kind, i): n * Q + q for n in range(N) for kind, i, q, _ in jobs.get(n, [])} for jobs in JOBS)
SOFT_STEP = (7, 13)
RMS_STEP = 10
NORM_STEP = 8


def build(nc, x, w_in, conv_w, conv_b, w_x, dt_ln, b_ln, c_ln, w_dt, dt_bias, a_mat, d_par, w_out, w_gu, w_dn,
          b_rows, wdn_rows, out):
    with ExitStack() as ctx:
        def sb(name, shape, dt=F32):
            return ctx.enter_context(nc.sbuf_tensor(name, shape, dt))

        def bank(name):
            return ctx.enter_context(nc.psum_tensor(name, [P, 512], F32))

        def sem(name):
            return ctx.enter_context(nc.semaphore(name))

        wx = sb("wx", [P, DT, SSM])
        wdt = sb("wdt", [DTR, D], F32R)
        cw = sb("cw", [P, DT, TAPS])
        cb = sb("cb", [P, DT])
        dtb = sb("dtb", [P, DT])
        dpar = sb("dpar", [P, DT])
        amat = sb("amat", [P, DT, N])
        lnw = sb("lnw", [P, SSM])
        ident = sb("ident", [P, P])
        minus_half = sb("minus_half", [P, TT * 3])
        win = sb("win", [P, 2, HT, P])
        wgu = sb("wgu", [P, 2, 2, HT, P], F16)
        wdn = sb("wdn", [P, 2, H], F32R)
        wout = sb("wout", [P, Q, H])
        brow = sb("brow", [P, 2, T])
        xin = sb("xin", [P, TT, H])
        acc = sb("acc", [P, TT, H])
        yT = sb("yT", [P, G, TT, Q * P])
        cn = sb("cn", [P, TT, N])
        xnT = sb("xnT", [P, HT, T])
        xhi = sb("xhi", [P, HT, T], F16)
        xlo = sb("xlo", [P, HT, T], F16)
        u = sb("u", [P, DT, T])
        gate = sb("gate", [P, DT, T])
        delta = sb("delta", [P, G, Q, T])
        du = sb("du", [P, G, Q, T])
        h = sb("h", [P, 2, Q, T])
        b = sb("b", [P, 2, Q, T])
        shared = sb("shared", [P, 3 * T + 2 * UP])
        conv = shared[:, 0:3 * T].rearrange("p (s t) -> p s t", t=T)
        upad = shared[:, 3 * T:3 * T + 2 * UP].rearrange("p (s t) -> p s t", t=UP)
        sig = sb("sig", [P, 2, T])
        ud = sb("ud", [P, 2, T])
        state = sb("state", [P, 2, DT, N])
        carry = sb("carry", [P, 2, DT, TAPS - 1])
        stats = sb("stats", [P, TT, 6])
        meanvar = sb("meanvar", [P, TT, 2])
        veps = sb("veps", [P, TT])
        rstd = sb("rstd", [P, TT])
        nmr = sb("nmr", [P, TT])
        ssn = sb("ssn", [P, TT, SSM])
        ms = sb("ms", [P, TT, 3])
        mse = sb("mse", [P, TT, 3])
        rms = sb("rms", [P, TT, 3])
        dtT = sb("dtT", [DTR, T], F32R)
        th = sb("th", [P, ST])
        v = sb("v", [P, ST])
        hf = sb("hf", [P, 2, ST])
        hhi = sb("hhi", [P, 2, ST], F32R)
        hlo = sb("hlo", [P, 2, ST], F32R)
        xn = shared[:, 0:TT * H].rearrange("p (t h) -> p t h", h=H)
        ss, sq, sw = (shared[:, i * TT * SSM:(i + 1) * TT * SSM].rearrange("p (t k) -> p t k", k=SSM) for i in range(3))
        dts = shared[:, 3 * TT * SSM:3 * TT * SSM + TT * (DTR + N)].rearrange("p (t k) -> p t k", k=DTR + N)
        bT = shared[0:DTR + N, UP * 3:UP * 3 + T]
        wdt_raw, wdt_rounded = (gate[0:DTR, 2 * i:2 * i + 2].rearrange("p s t -> p (s t)") for i in range(2))
        wdn16 = yT[:].rearrange("p g t d -> p (g t d)").bitcast(F16)[:, 0:MT * H]
        HALF = MT // 2 * H
        wdn_stage = [z[:].rearrange("p g q t -> p (g q t)")[:, 0:HALF] for z in (delta, du)]

        pA = [bank(f"pA{i}") for i in range(2)]
        pT = [bank(f"pT{i}") for i in range(2)]
        pG = bank("pG")
        pO = [bank(f"pO{i}") for i in range(SB)]
        pX = bank("pX")

        s_const, s_wdn16, s_x = sem("consts_in"), sem("wdn16_in"), sem("x_in")
        s_win, s_gu, s_wd, s_brow = ([sem(f"{n}{i}") for i in range(2)] for n in ("win_in", "gu_in", "wdn_in", "brow_in"))
        s_wo, s_brows, s_out, s_stored = sem("wout_in"), sem("b_rows_stored"), sem("out_stored"), sem("wdn_stored")
        s_zeroed, s_ident, s_half, s_wdn, s_passed = (sem(n) for n in (
            "zeroed", "ident_done", "half_done", "wdn_rounded", "passed"))
        s_full, s_read = sem("side_bank_full"), sem("side_bank_read")
        s_stats, s_mv, s_veps, s_rstd, s_nmr, s_xn, s_xhi, s_xlo, s_acc = (sem(n) for n in (
            "stats", "meanvar", "veps", "rstd", "minus_mean_rstd", "xn", "x_high", "x_low", "acc_is_x"))
        s_head, s_upad, s_conv, s_tail, s_tanh_side, s_sig, s_silu = (sem(n) for n in (
            "upad_head", "upad_tile", "tap_added", "carry_kept", "side_tanh", "sigmoid", "silu"))
        s_ss, s_ms, s_mse, s_rms, s_sw, s_ssn, s_cn = (sem(n) for n in (
            "ss", "mean_squares", "ms_eps", "rms", "ss_weighted", "ss_normed", "c_kept"))
        s_dts, s_wdt = sem("dt_parts"), sem("w_dt_parts")
        s_relu, s_soft, s_ud = (sem(n) for n in ("z_relu", "soft", "u_d"))
        s_delta, s_du = ([sem(f"{n}_half{i}") for i in range(2)] for n in ("delta", "du"))
        s_b, s_keep, s_exp, s_scan, s_hT, s_stt = (sem(n) for n in (
            "b_done", "state_kept", "exp_done", "scan_done", "h_turned", "y_added"))
        s_up, s_tanh, s_v, s_hf, s_hhi, s_hlo, s_down, s_ffn = (sem(n) for n in (
            "up_done", "tanh_done", "v_done", "hf_done", "hhi_done", "hlo_done", "down_done", "ffn_added"))

        RING, ONE, BROW0 = 2, 1, 4
        N_SIDE = (len(ORDER[0]), len(ORDER[1]))

        def job(c, g, kind, i):
            return (c + 1) * sum(N_SIDE) + (N_SIDE[0] if g else 0) + ORDER[g].index((kind, i))

        def filled(k):
            return k + 1

        def emptied(k):
            return k + 1 + ONE

        def alone(c):
            return isinstance(c, int) and (c < 0 or c == CHUNKS)

        def bank_of(c, k):
            return (pX, pT[0])[k % 2] if alone(c) else pX

        def of_phase(ph, n, q=0, count=1):
            return ph * (N * count) + n * count + q + 1

        def unit(ph, n):
            return ph * MT + n + 1

        def silu(c, g, j):
            return (c + g) * (2 * DT) + (0 if g else DT) + j

        def phases(eng, phase):
            phase(-1, 0, False, False, False, True)
            phase(-1, 1, False, False, True, False)
            phase(0, 0, True, False, True, True)
            with eng.Fori(0, CHUNKS - 2) as c:
                phase(c, 1, True, True, True, False)
                phase(c + 1, 0, True, True, True, True)
            phase(CHUNKS - 2, 1, True, True, True, False)
            phase(CHUNKS - 1, 0, True, True, True, False)
            phase(CHUNKS - 1, 1, True, True, False, False)
            phase(CHUNKS, 0, False, True, False, False)

        def at_quarter(g, n, q):
            return [(kind, i, (m - n) * Q + q0, (m - n) * Q + q1) for m in range(n + 1)
                    for kind, i, q0, q1 in JOBS[g].get(m, []) if m * Q + q0 <= n * Q + q <= m * Q + q1]

        def missing(g, n, q, post, work, ahead):
            return [(kind, i) for m in range(N) for kind, i, _, last in JOBS[g].get(m, [])
                    if m * Q + last + 1 == n * Q + q and not does(kind, post, work, ahead)]

        def does(kind, post, work, ahead):
            return post if kind in ("YT", "WO") else ahead if kind == "XT" else work

        def ended(g, n, q, post, work, ahead):
            return [(kind, i) for m in range(N) for kind, i, _, last in JOBS[g].get(m, [])
                    if m * Q + last + 1 == n * Q + q and does(kind, post, work, ahead)]

        def scan_before(c, g):
            return not (isinstance(c, int) and c * G + g < 1)

        def make_delta(eng, p, pg, half):
            qs = slice(half * (Q // 2), (half + 1) * (Q // 2))
            eng.wait_ge(s_soft, p * 3 + 3)
            eng.tensor_tensor(delta[:, pg, qs], delta[:, pg, qs], du[:, pg, qs], ALU.add).then_inc(s_delta[half], 1)

        def make_du(eng, p, pg, half):
            lo = half * (Q // 2)
            eng.wait_ge(s_delta[half], p + 1)
            eng.tensor_tensor(du[:, pg, lo:lo + Q // 2], delta[:, pg, lo:lo + Q // 2],
                              u[:, pg * Q + lo:pg * Q + lo + Q // 2], ALU.mult).then_inc(s_du[half], 1)

        def plain(eng):
            eng.sem_inc(s_passed, 1)

        consts = [(wx[:], w_x), (cw[:], conv_w), (cb[:], conv_b), (dtb[:], dt_bias),
                  (dpar[:], d_par), (amat[:], a_mat), (lnw[:, 0:R], dt_ln.partition_broadcast(P)),
                  (lnw[:, R:R + N], b_ln.partition_broadcast(P)), (lnw[:, R + N:SSM], c_ln.partition_broadcast(P))]
        consts += [(wdt_raw[i * R:(i + 1) * R], w_dt) for i in range(3)]
        block = ctx.enter_context(nc.Block())

        @block.sync
        def _(sp):
            sp.dma_start(xin[:], x[0]).then_inc(s_x, 16)
            sp.dma_start(win[:, 0], w_in[0, 0]).then_inc(s_win[0], 16)
            for tile, dram in consts:
                sp.dma_start(tile, dram).then_inc(s_const, 16)
            sp.dma_start(wdn16, w_dn).then_inc(s_wdn16, 16)
            sp.sem_inc(s_out, 16)

            def load_win(c, g, j):
                k = silu(c, g, j)
                part = 0 if g else 1
                if not (isinstance(k, int) and k < 2):
                    before = (c, g, j - 2) if j >= 2 else (c, 0, j + DT - 2) if g else (c - 1, 1, j + DT - 2)
                    kind = "UT" if before[1] else "GT"
                    sp.wait_ge(s_full, filled(job(*before[:2], kind, before[2])))
                sp.dma_start(win[:, j % 2], w_in[j, part]).then_inc(s_win[j % 2], 16)

            def load_brow(c, g, n):
                ph = c * G + g
                sp.wait_ge(s_b, of_phase(ph, n - 2, 1, 2) + BROW0)
                sp.dma_start(brow[:, n % 2], b_rows[c, n].partition_broadcast(P)).then_inc(s_brow[n % 2], 16)

            def load_up(ph, n):
                sp.wait_ge(s_up, unit(ph, n - 2) + RING)
                sp.dma_start(wgu[:, n % 2], w_gu[n]).then_inc(s_gu[n % 2], 16)

            def load_down(ph, n):
                sp.wait_ge(s_down, unit(ph, n - 2) + RING)
                sp.dma_start(wdn[:, n % 2].bitcast(F32), wdn_rows[n]).then_inc(s_wd[n % 2], 16)

            def phase(c, g, scan, post, work, ahead):
                ph = c * G + g
                tiles = {STEP_OF[g][("UT" if g else "GT", j)]: j for j in range(DT)} if work else {}
                for n in range(-1, N):
                    if n == -1 and scan:
                        load_up(ph, 0)
                    if n == -1 and scan and ahead:
                        sp.wait_ge(s_xn, (c + 1) * TT)
                        plain(sp)
                        sp.dma_start(xin[:], x[c + 1]).then_inc(s_x, 16)
                    if n == -1 and post:
                        if not (isinstance(c, int) and (c, g) == (0, 1)):
                            sp.wait_ge(s_full, filled(job(c, 0, "WO", Q - 1) if g else job(c - 1, 1, "WO", Q - 1)))
                        first = 0 if g else Q
                        sp.dma_start(wout[:], w_out[:, first:first + Q]).then_inc(s_wo, 16)
                    if scan and n + 1 < N and n >= 0:
                        load_brow(c, g, n + 1)
                    if scan and 0 <= n and n + 1 < MT:
                        load_up(ph, n + 1)
                    if n >= 0 and n + 1 in tiles:
                        load_win(c, g, tiles[n + 1])
                    if scan and 0 <= n - 1 < MT:
                        if n == 1 and isinstance(ph, int) and ph == 0:
                            sp.wait_ge(s_stored, 32)
                        load_down(ph, n - 1)
                    if n == DT - 1 and isinstance(c, int) and (c, g) == (-1, 1):
                        sp.wait_ge(s_wdn, 2)
                        for i in range(2):
                            sp.dma_start(wdn_rows[i * (MT // 2):(i + 1) * (MT // 2)].rearrange("m p h -> p m h"),
                                         wdn_stage[i].rearrange("p (m h) -> p m h", h=H)).then_inc(s_stored, 16)
                    if n == STEP_OF[1][("DTT", 0)] + 1 and g == 1 and work:
                        sp.wait_ge(s_read, emptied(job(c, 1, "DTT", 0)))
                        sp.dma_start(b_rows[c + 1], bT[DTR:DTR + N]).then_inc(s_brows, 16)
                    if n == N - 1 and work:
                        if g == 1:
                            sp.wait_ge(s_brows, (c + 2) * 16)
                            plain(sp)
                        load_brow(*((c + 1, 0) if g else (c, 1)), 0)
                    if n == N - 1 and g == 0 and ahead and not (isinstance(c, int) and c < 0):
                        load_win(c, 1, 0)
                    if n == N - 1 and g == 1 and work:
                        load_win(c + 1, 0, 0)
                    if alone(c) and c == CHUNKS and n - 1 in range(2, 6):
                        t = n - 3
                        sp.wait_ge(s_read, emptied(job(c, 0, "WO", t)))
                        sp.dma_start(out[c - 1][:, t], acc[:, t]).then_inc(s_out, 16)
                    if post and g == 0 and not alone(c) and n == STEP_OF[0][("WO", Q - 1)] + 2:
                        sp.wait_ge(s_read, emptied(job(c, 0, "WO", Q - 1)))
                        sp.dma_start(out[c - 1], acc[:]).then_inc(s_out, 16)
                    if scan and g == 0 and n == STEP_OF[0][("WO", Q - 1)] + 4:
                        sp.wait_ge(s_out, (c + 1) * 16)
                        plain(sp)
                        sp.dma_start(acc[:], x[c]).then_inc(s_acc, 16)
                plain(sp)
            phases(sp, phase)
            sp.wait_ge(s_out, (CHUNKS + TT) * 16)

        @block.gpsimd
        def _(pool):
            pool.sem_inc(s_b, BROW0)
            pool.sem_inc(s_keep, RING)
            pool.sem_inc(s_silu, RING)
            pool.sem_inc(s_hlo, RING)
            pool.memset(ident[:], 0.0).then_inc(s_zeroed, 1)
            pool.memset(state[:], 0.0).then_inc(s_zeroed, 1)
            pool.memset(carry[:], 0.0).then_inc(s_zeroed, 1)
            pool.memset(minus_half[:], -0.5).then_inc(s_half, 1)
            pool.wait_ge(s_zeroed, 3)
            pool.affine_select(out=ident[:], in_=ident[:], compare_op=ALU.not_equal, fill=1.0, base=0,
                               pattern=[[-1, P]], channel_multiplier=1).then_inc(s_ident, 1)
            pool.wait_ge(s_half, 1)

            def make_b(c, g, n, half):
                ph = c * G + g
                if half == 0:
                    pool.wait_ge(s_brow[n % 2], (ph * (N // 2) + n // 2 + 1) * 16)
                qs = slice(half * (Q // 2), (half + 1) * (Q // 2))
                pool.tensor_tensor(b[:, n % 2, qs], du[:, g, qs], brow[:, n % 2].unsqueeze(1).broadcast_to([P, Q // 2, T]),
                                   ALU.mult).then_inc(s_b, 1)

            def keep_state(ph, g, n):
                pool.wait_ge(s_scan, of_phase(ph, n, Q - 1, Q) + RING)
                plain(pool)
                pool.tensor_copy(state[:, 1, g * Q:(g + 1) * Q, n:n + 1], h[:, n % 2, :, T - 1:T]).then_inc(s_keep, 1)

            def phase(c, g, scan, post, work, ahead):
                ph = c * G + g
                cc = c + 1

                def between(n):
                    if g == 1 and work:
                        j = n - STEP_OF[1][("UT", 0)]
                        if 0 < j <= DT:
                            pool.wait_ge(s_head, cc * DT + j)
                            pool.wait_ge(s_upad, cc * DT + j)
                            plain(pool)
                            pool.tensor_copy(carry[:, 1, j - 1], upad[:, (j - 1) % 2, T:UP]).then_inc(s_tail, 1)
                        if 0 <= j < DT:
                            if j == 0:
                                pool.wait_ge(s_full, filled(job(c, 0, "XT", HT - 1)))
                            if j >= 2:
                                pool.wait_ge(s_conv, (cc * DT + j - 1) * (TAPS - 1))
                            plain(pool)
                            pool.tensor_copy(upad[:, j % 2, 0:TAPS - 1], carry[:, cc % 2, j]).then_inc(s_head, 1)
                        if n == RMS_STEP:
                            pool.wait_ge(s_mse, (cc + 1) * 2)
                            pool.tensor_tensor(rms[:].rearrange("p t k -> p (t k)"),
                                               mse[:].rearrange("p t k -> p (t k)"), minus_half[:],
                                               ALU.pow).then_inc(s_rms, 1)
                        if 0 <= j - 2 < DT:
                            k = silu(c, 1, j - 2)
                            pool.wait_ge(s_sig, k + 1)
                            pool.tensor_tensor(u[:, j - 2], conv[:, (j - 2) % 3], sig[:, (j - 2) % 2], ALU.mult).then_inc(s_silu, 1)
                    if g == 0 and work:
                        for j in range(DT):
                            if STEP_OF[0][("GT", j)] == n - 2:
                                k = silu(c, 0, j)
                                pool.wait_ge(s_sig, k + 1)
                                pool.tensor_tensor(gate[:, j], gate[:, j], sig[:, j % 2], ALU.mult).then_inc(s_silu, 1)

                if scan_before(c, g):
                    keep_state(ph - 1, 1 - g, N - 1)
                for n in range(N):
                    if scan and n >= 1:
                        keep_state(ph, g, n - 1)
                    for half in range(2):
                        if half == 1:
                            between(n)
                            if ahead and n == NORM_STEP:
                                pool.wait_ge(s_veps, cc + 1)
                                pool.tensor_tensor(rstd[:], veps[:], minus_half[:, 0:TT], ALU.pow).then_inc(s_rstd, 1)
                        if n + 1 < N and scan:
                            make_b(c, g, n + 1, half)
                        if n + 1 == N and work:
                            pool.wait_ge(s_du[half], ph + 2)
                            make_b(*((c + 1, 0) if g else (c, 1)), 0, half)
                    if scan and 1 <= n <= MT:
                        pool.wait_ge(s_hhi, unit(ph, n - 1))
                        pool.wait_ge(s_down, unit(ph, n - 3) + RING)
                        pool.tensor_tensor(hlo[:, (n - 1) % 2], hf[:, (n - 1) % 2], hhi[:, (n - 1) % 2].bitcast(F32),
                                           ALU.subtract).then_inc(s_hlo, 1)
                    if scan and work and g == 1 and n == SOFT_STEP[1] + 1:
                        make_delta(pool, ph + 1, 0, 1)
                        make_du(pool, ph + 1, 0, 1)
                    if scan and work and g == 1 and n == N - 1:
                        pool.wait_ge(s_xhi, cc + 1)
                        pool.tensor_tensor(xlo[:, HT // 2:], xnT[:, HT // 2:], xhi[:, HT // 2:], ALU.subtract).then_inc(s_xlo, 1)
                plain(pool)
            phases(pool, phase)

        @block.scalar
        def _(act):
            act.sem_inc(s_read, ONE)

            def phase(c, g, scan, post, work, ahead):
                ph = c * G + g
                cc = c + 1
                nph, ng = ph + 1, 1 - g

                def empty(kind, i):
                    k = job(c, g, kind, i)
                    pX = bank_of(c, k)
                    act.wait_ge(s_full, filled(k))
                    if kind == "XT":
                        act.copy(xnT[:, i], pX[:]).then_inc(s_read, 1)
                    elif kind == "UT":
                        if i >= 2:
                            act.wait_ge(s_tail, cc * DT + i - 1)
                            act.wait_ge(s_conv, (cc * DT + i - 1) * (TAPS - 1))
                        if i >= 3:
                            act.wait_ge(s_silu, silu(c, 1, i - 3) + 1 + RING)
                        act.copy(upad[:, i % 2, TAPS - 1:UP], pX[:]).then_inc(s_read, 1)
                        act.wait_ge(s_read, emptied(k))
                        act.activation(conv[:, i % 3], upad[:, i % 2, TAPS - 1:UP], ACT.Identity, bias=cb[:, i:i + 1],
                                       scale=cw[:, i, TAPS - 1:TAPS]).then_inc(s_upad, 1)
                    elif kind == "GT":
                        act.copy(gate[:, i], pX[:]).then_inc(s_read, 1)
                    elif kind == "SSM":
                        act.copy(shared[:, 0:TT * SSM], pX[:, 0:TT * SSM]).then_inc(s_ss, 1)
                        act.activation(shared[:, TT * SSM:2 * TT * SSM], pX[:, 0:TT * SSM],
                                       ACT.Square).then_inc(s_read, 1)
                    elif kind == "DTT":
                        act.copy(dtT[:], pX[0:DTR, :])
                        act.copy(bT[DTR:DTR + N], pX[DTR:DTR + N, :]).then_inc(s_read, 1)
                    elif kind == "Z":
                        act.activation(du[:, ng, i], pX[:], ACT.Relu,
                                       bias=dtb[:, ng * Q + i:ng * Q + i + 1]).then_inc(s_relu, 1)
                        act.activation(delta[:, ng, i], pX[:], ACT.Abs,
                                       bias=dtb[:, ng * Q + i:ng * Q + i + 1]).then_inc(s_read, 1)
                    elif kind == "UD":
                        act.copy(yT[:, ng, :, i * P:(i + 1) * P],
                                 pX[:].rearrange("p (t d) -> p t d", d=P)).then_inc(s_read, 1)

                def skip(n, q):
                    for kind, i in missing(g, n, q, post, work, ahead):
                        act.wait_ge(s_full, filled(job(c, g, kind, i)))
                        act.wait_ge(s_read, emptied(job(c, g, kind, i) - 1))
                        act.sem_inc(s_read, 1)

                def decay(p, pg, n, q):
                    act.wait_ge(s_scan, of_phase(p, n, q - 2, Q) + RING)
                    j = pg * Q + q
                    act.activation(pA[q % 2][:], delta[:, pg, q], ACT.Exp, scale=amat[:, j, n:n + 1]).then_inc(s_exp, 1)

                def scale_u(i):
                    j = ng * Q + i
                    act.wait_ge(s_silu, (silu(c, 1, j) if g else silu(c - 1, 1, j)) + 1 + RING)
                    if i >= 2:
                        act.wait_ge(s_full, filled(job(c, g, "UD", i - 2)))
                    act.activation(ud[:, i % 2], u[:, j], ACT.Copy, scale=dpar[:, j:j + 1]).then_inc(s_ud, 1)

                for n in range(N):
                    if isinstance(c, int) and (c, g) == (-1, 1) and n == 0:
                        act.wait_ge(s_const, 16 * len(consts))
                    if isinstance(c, int) and (c, g) == (-1, 1) and n == STEP_OF[1][("Z", 0)]:
                        act.wait_ge(s_stored, 32)
                    for q in range(Q):
                        if scan and (n, q) != (N - 1, Q - 1):
                            decay(ph, g, n + (q + 1) // Q, (q + 1) % Q)
                        i = {STEP_OF[0][("GT", i)] + 1: i for i in range(DT)}.get(n) if g == 0 and work else None
                        if i is not None and q == 1:
                            act.wait_ge(s_silu, silu(c, 0, i) - 2 + 1 + RING)
                            act.wait_ge(s_read, emptied(job(c, 0, "GT", i)))
                            act.activation(sig[:, i % 2], gate[:, i], ACT.Tanh, scale=0.5).then_inc(s_tanh_side, 1)
                        if i is not None and q == 2:
                            act.wait_ge(s_tanh_side, silu(c, 0, i) + 1)
                            act.activation(sig[:, i % 2], sig[:, i % 2], ACT.Copy, scale=0.5, bias=0.5).then_inc(s_sig, 1)
                        if work and (n, q) == (N - 1, Q - 1):
                            for half in range(2):
                                act.wait_ge(s_delta[half], nph + 1)
                            decay(nph, ng, 0, 0)
                        if scan and q == 3 and n < MT:
                            act.wait_ge(s_up, unit(ph, n) + RING)
                            act.activation(th[:], pG[:, 0:ST], ACT.Tanh, scale=0.5).then_inc(s_tanh, 1)
                        if isinstance(c, int) and c < 0:
                            skip(n, q)
                        for kind, i in ended(g, n, q, post, work, ahead):
                            if kind not in ("YT", "WO"):
                                empty(kind, i)
                        if scan and q == 1 and 1 <= n <= MT:
                            act.wait_ge(s_hf, unit(ph, n - 1) + ONE)
                            act.wait_ge(s_down, unit(ph, n - 3) + RING)
                            act.copy(hhi[:, (n - 1) % 2], hf[:, (n - 1) % 2]).then_inc(s_hhi, 1)
                        if ahead and n == NORM_STEP + 1:
                            act.wait_ge(s_nmr, cc + 1)
                            act.activation(xn[:, q], xin[:, q], ACT.Identity, bias=nmr[:, q:q + 1],
                                           scale=rstd[:, q:q + 1]).then_inc(s_xn, 1)
                        if g == 1 and work and q < 2:
                            j = n - 2 - STEP_OF[1][("UT", 0)]
                            k = silu(c, 1, j)
                            if 0 <= j < DT and q == 0:
                                act.wait_ge(s_conv, (cc * DT + j + 1) * (TAPS - 1))
                                act.wait_ge(s_silu, k - 2 + 1 + RING)
                                act.activation(sig[:, j % 2], conv[:, j % 3], ACT.Tanh, scale=0.5).then_inc(s_tanh_side, 1)
                            if 0 <= j < DT and q == 1:
                                act.wait_ge(s_tanh_side, k + 1)
                                act.activation(sig[:, j % 2], sig[:, j % 2], ACT.Copy, scale=0.5, bias=0.5).then_inc(s_sig, 1)
                        if work and n == SOFT_STEP[g] and q < 2:
                            qs = slice(q * (Q // 2), (q + 1) * (Q // 2))
                            if q == 0:
                                act.wait_ge(s_read, emptied(job(c, g, "Z", Q - 1)))
                            act.activation(delta[:, ng, qs], delta[:, ng, qs], ACT.Exp, scale=-1.0).then_inc(s_soft, 1)
                        if work and (n, q) == (SOFT_STEP[g], 2):
                            act.wait_ge(s_soft, nph * 3 + 2)
                            act.activation(delta[:, ng], delta[:, ng], ACT.Ln, bias=1.0).then_inc(s_soft, 1)
                        if g == 1 and work and (n, q) == (N - 2 if scan else DT - 1, 3):
                            if scan:
                                act.wait_ge(s_up, unit(ph, MT - 1) + RING)
                            act.copy(xhi[:], xnT[:]).then_inc(s_xhi, 1)
                        for i in range(Q):
                            if work and n * Q + q + 2 == QUARTER_OF[g][("UD", i)]:
                                scale_u(i)
                if isinstance(c, int) and c < 0:
                    skip(N, 0)
                for kind, i in ended(g, N, 0, post, work, ahead):
                    empty(kind, i)
                plain(act)
            phases(act, phase)

        @block.vector
        def _(dve):
            for s, start in ((s_scan, RING), (s_stt, RING), (s_hf, ONE), (s_ffn, ONE)):
                dve.sem_inc(s, start)

            def prepare():
                dve.wait_ge(s_const, 16 * len(consts))
                dve.tensor_copy(wdt_rounded[2 * R:DTR].bitcast(F32R), wdt_raw[2 * R:DTR]).then_inc(s_wdt, 1)
                dve.tensor_copy(wdt[0:2 * R], wdt_raw[0:2 * R]).then_inc(s_wdt, 1)
                dve.wait_ge(s_wdt, 2)
                dve.tensor_tensor(wdt[2 * R:DTR], wdt_raw[2 * R:DTR], wdt_rounded[2 * R:DTR], ALU.subtract).then_inc(s_wdt, 1)
                dve.wait_ge(s_wdn16, 16)
                for i in range(2):
                    dve.tensor_copy(wdn_stage[i], wdn16[:, i * HALF:(i + 1) * HALF]).then_inc(s_wdn, 1)

            def phase(c, g, scan, post, work, ahead):
                ph = c * G + g
                cc = c + 1
                nph, ng = ph + 1, 1 - g

                def add_y(p, pg, n, t):
                    dve.wait_ge(s_hT, of_phase(p, n, t, TT))
                    dve.scalar_tensor_tensor(yT[:, pg, t], pT[t % 2][:], cn[:, t, n:n + 1], yT[:, pg, t],
                                             ALU.mult, ALU.add).then_inc(s_stt, 1)

                def empty(kind, i):
                    k = job(c, g, kind, i)
                    pX = bank_of(c, k)
                    if kind == "YT":
                        j = ng * Q + i
                        dve.wait_ge(s_full, filled(k))
                        dve.wait_ge(s_silu, (silu(c, 0, j) if g else silu(c - 1, 0, j)) + 1 + RING)
                        dve.tensor_tensor(gate[:, j], pX[:], gate[:, j], ALU.mult).then_inc(s_read, 1)
                    elif kind == "WO":
                        dve.wait_ge(s_full, filled(k))
                        if i == 0:
                            dve.wait_ge(s_ffn, ph * SB + ONE)
                        dve.tensor_tensor(acc[:, i], acc[:, i], pX[:], ALU.add).then_inc(s_read, 1)

                def rms_sums():
                    parts = [(0, R), (R, R + N), (R + N, SSM)]
                    dve.wait_ge(s_ss, cc + 1)
                    dve.wait_ge(s_read, emptied(job(c, g, "SSM", 0)))
                    for i, (lo, hi) in enumerate(parts):
                        dve.tensor_reduce(ms[:, :, i:i + 1], sq[:, :, lo:hi], AX.X, ALU.add).then_inc(s_ms, 1)
                    dve.tensor_tensor(sw[:], ss[:], lnw[:].unsqueeze(1).broadcast_to([P, TT, SSM]),
                                      ALU.mult).then_inc(s_sw, 1)
                    dve.wait_ge(s_ms, (cc + 1) * 3)
                    dve.tensor_scalar(mse[:, :, 0:1], ms[:, :, 0:1], 1.0 / R, RMS_EPS, ALU.mult, ALU.add).then_inc(s_mse, 1)
                    dve.tensor_scalar(mse[:, :, 1:3], ms[:, :, 1:3], 1.0 / N, RMS_EPS, ALU.mult, ALU.add).then_inc(s_mse, 1)

                def rms_norms():
                    parts = [(0, R), (R, R + N), (R + N, SSM)]
                    dve.wait_ge(s_rms, cc + 1)
                    dve.wait_ge(s_sw, cc + 1)
                    for i, (lo, hi) in enumerate(parts):
                        to = dts[:, :, DTR:DTR + N] if i == 1 else ssn[:, :, lo:hi]
                        dve.tensor_tensor(to, sw[:, :, lo:hi],
                                          rms[:, :, i:i + 1].broadcast_to([P, TT, hi - lo]), ALU.mult).then_inc(s_ssn, 1)
                    dve.wait_ge(s_ssn, cc * 3 + 1)
                    dve.tensor_copy(dts[:, :, 0:R].bitcast(F32R), ssn[:, :, 0:R]).then_inc(s_dts, 1)
                    dve.tensor_copy(dts[:, :, 2 * R:DTR].bitcast(F32R), ssn[:, :, 0:R]).then_inc(s_dts, 1)
                    dve.wait_ge(s_dts, cc * 3 + 1)
                    dve.tensor_tensor(dts[:, :, R:2 * R], ssn[:, :, 0:R], dts[:, :, 0:R], ALU.subtract).then_inc(s_dts, 1)

                if isinstance(c, int) and (c, g) == (-1, 1):
                    prepare()
                for n in range(N):
                    if ahead and n == NORM_STEP:
                        dve.wait_ge(s_x, (cc + 1) * 16)
                        for t in range(TT):
                            dve.bn_stats(stats[:, t], xin[:, t]).then_inc(s_stats, 1)
                        for t in range(TT):
                            dve.wait_ge(s_stats, cc * TT + t + 1)
                            plain(dve)
                            dve.bn_aggr(meanvar[:, t], stats[:, t]).then_inc(s_mv, 1)
                        dve.wait_ge(s_mv, (cc + 1) * TT)
                        dve.tensor_scalar(veps[:], meanvar[:, :, 1], LN_EPS, None, ALU.add).then_inc(s_veps, 1)
                    for q in range(Q):
                        if scan:
                            if q == 0:
                                dve.wait_ge(s_keep, of_phase(ph, n - 2) + RING)
                            if q % 2 == 0:
                                dve.wait_ge(s_b, of_phase(ph, n, q // 2, 2) + BROW0)
                            dve.wait_ge(s_exp, of_phase(ph, n, q, Q))
                            j = g * Q + q
                            dve.tensor_tensor_scan(h[:, n % 2, q], pA[q % 2][:], b[:, n % 2, q],
                                                   state[:, c % HALVES, j, n:n + 1], ALU.mult, ALU.add).then_inc(s_scan, 1)
                        if scan and 1 <= n <= MT and q == 0:
                            dve.wait_ge(s_tanh, unit(ph, n - 1))
                            dve.scalar_tensor_tensor(v[:], th[:], 1.0, pG[:, ST:2 * ST], ALU.add, ALU.mult).then_inc(s_v, 1)
                        if n == 0 and scan_before(c, g):
                            add_y(ph - 1, 1 - g, N - 1, q)
                        if n >= 1 and scan:
                            if n == 1 and q == 0:
                                dve.wait_ge(s_cn, c + 1)
                                dve.wait_ge(s_read, emptied(job(c - 1, 1, "UD", Q - 1) if g == 0 else job(c, 0, "UD", Q - 1)))
                            add_y(ph, g, n - 1, q)
                        if scan and 1 <= n <= MT and q == 0:
                            dve.wait_ge(s_v, unit(ph, n - 1))
                            dve.wait_ge(s_hlo, unit(ph, n - 3) + RING)
                            dve.scalar_tensor_tensor(hf[:, (n - 1) % 2], pG[:, 0:ST], 0.5, v[:],
                                                     ALU.mult, ALU.mult).then_inc(s_hf, 1)
                        if isinstance(c, int) and c == CHUNKS:
                            for kind, i in missing(g, n, q, post, work, ahead):
                                dve.wait_ge(s_full, filled(job(c, g, kind, i)))
                                dve.wait_ge(s_read, emptied(job(c, g, kind, i) - 1))
                                dve.sem_inc(s_read, 1)
                        for kind, i in ended(g, n, q, post, work, ahead):
                            empty(kind, i)
                        if ahead and n == NORM_STEP and q == 3:
                            dve.wait_ge(s_rstd, cc + 1)
                            dve.scalar_tensor_tensor(nmr[:], meanvar[:, :, 0], -1.0, rstd[:], ALU.mult, ALU.mult).then_inc(s_nmr, 1)
                        if g == 1 and work:
                            j = n - 1 - STEP_OF[1][("UT", 0)]
                            if 0 <= j < DT and q >= 1:
                                if q == 1:
                                    dve.wait_ge(s_head, cc * DT + j + 1)
                                    dve.wait_ge(s_upad, cc * DT + j + 1)
                                else:
                                    dve.wait_ge(s_conv, (cc * DT + j) * (TAPS - 1) + q - 1)
                                dve.scalar_tensor_tensor(conv[:, j % 3], upad[:, j % 2, q - 1:q - 1 + T], cw[:, j, q - 1:q],
                                                         conv[:, j % 3], ALU.mult, ALU.add).then_inc(s_conv, 1)
                            if n == RMS_STEP and q == 1:
                                rms_sums()
                            if n == RMS_STEP and q == 3:
                                rms_norms()
                            if (n, q) == (N - 1 if scan else DT, 0):
                                dve.wait_ge(s_xhi, cc + 1)
                                for ks in [slice(0, HT // 2)] + ([] if scan else [slice(HT // 2, HT)]):
                                    dve.tensor_tensor(xlo[:, ks], xnT[:, ks], xhi[:, ks], ALU.subtract).then_inc(s_xlo, 1)
                        if work and g == 0 and 0 <= n - SOFT_STEP[0] - 2 < 4 and q == 2:
                            what, half = divmod(n - SOFT_STEP[0] - 2, 2)
                            if what == 0:
                                make_delta(dve, nph, 1, half)
                            else:
                                make_du(dve, nph, 1, half)
                        if work and g == 1 and (n, q) == (SOFT_STEP[1] + 1, 0):
                            for half in range(1 if scan else 2):
                                make_delta(dve, nph, 0, half)
                                make_du(dve, nph, 0, half)
                    if scan and g == 0 and n == 0:
                        dve.wait_ge(s_stt, of_phase(ph - 1, N - 1, TT - 1, TT) + RING)
                        dve.wait_ge(s_ssn, (c + 1) * 3)
                        plain(dve)
                        dve.tensor_copy(cn[:], ssn[:, :, R + N:SSM]).then_inc(s_cn, 1)
                if scan:
                    dve.wait_ge(s_down, unit(ph, MT - 1) + RING)
                    dve.wait_ge(s_acc, (c + 1) * 16)
                    if g == 1:
                        dve.wait_ge(s_read, emptied(job(c, 1, "WO", Q - 1)))
                    for t in range(SB):
                        dve.tensor_tensor(acc[:, g * SB + t], acc[:, g * SB + t], pO[t][:], ALU.add).then_inc(s_ffn, 1)
                plain(dve)
            phases(dve, phase)

        @block.tensor
        def _(pe):
            pe.sem_inc(s_up, RING)
            pe.sem_inc(s_down, RING)
            pe.wait_ge(s_ident, 1)

            def phase(c, g, scan, post, work, ahead):
                ph = c * G + g
                cc = c + 1
                ng = 1 - g

                def turn_h(p, n, t):
                    if t == 0:
                        pe.wait_ge(s_scan, of_phase(p, n, Q - 1, Q) + RING)
                    pe.wait_ge(s_stt, of_phase(p, n, t - 2, TT) + RING)
                    for q in range(Q):
                        last = pe.transpose(pT[t % 2][:, q * P:(q + 1) * P], h[:, n % 2, q, t * P:(t + 1) * P], ident[:])
                    last.then_inc(s_hT, 1)

                def up(n, part):
                    if part == 0:
                        pe.wait_ge(s_gu[n % 2], (ph * (MT // 2) + n // 2 + 1) * 16)
                        pe.wait_ge(s_hf, unit(ph, n - 1) + ONE)
                    for k in range(HT):
                        for xx in (xhi, xlo):
                            last = pe.matmul(pG[:, part * ST:(part + 1) * ST], wgu[:, n % 2, part, k],
                                             xx[:, k, g * ST:(g + 1) * ST], start=(k == 0 and xx is xhi),
                                             stop=(k == HT - 1 and xx is xlo))
                    if part == 1:
                        last.then_inc(s_up, 1)

                def down(n):
                    if n == 0:
                        pe.wait_ge(s_ffn, ph * SB + ONE)
                    pe.wait_ge(s_wd[n % 2], (ph * (MT // 2) + n // 2 + 1) * 16)
                    pe.wait_ge(s_hlo, unit(ph, n) + RING)
                    for t in range(SB):
                        for hh in (hhi, hlo):
                            last = pe.matmul(pO[t][:], hh[:, n % 2, t * P:(t + 1) * P], wdn[:, n % 2],
                                             start=(n == 0 and hh is hhi), stop=(n == MT - 1 and hh is hlo))
                    last.then_inc(s_down, 1)

                def side(kind, i, k, part, parts):
                    first, last = part == 0, None
                    pX = bank_of(c, k)
                    if kind in ("UT", "GT"):
                        if first and kind == "UT" and i == 0:
                            pe.wait_ge(s_read, emptied(job(c, 0, "XT", HT - 1)))
                        if first:
                            pe.wait_ge(s_win[i % 2], (silu(c, g, i) // 2 + 1) * 16)
                        for m in range(HT * part // parts, HT * (part + 1) // parts):
                            last = pe.matmul(pX[:], win[:, i % 2, m], xnT[:, m], start=(m == 0), stop=(m == HT - 1))
                    elif kind == "WO":
                        if first and i == 0:
                            pe.wait_ge(s_read, emptied(job(c, g, "YT", Q - 1)))
                            pe.wait_ge(s_wo, ph * 16)
                        for m in range(Q * part // parts, Q * (part + 1) // parts):
                            last = pe.matmul(pX[:], gate[:, ng * Q + m, i * P:(i + 1) * P], wout[:, m],
                                             start=(m == 0), stop=(m == Q - 1))
                    elif kind == "SSM":
                        for m in range(DT * part // parts, DT * (part + 1) // parts):
                            pe.wait_ge(s_silu, silu(c, 1, m) + 1 + RING)
                            for t in range(TT):
                                last = pe.matmul(pX[:, t * SSM:(t + 1) * SSM], u[:, m, t * P:(t + 1) * P], wx[:, m],
                                                 start=(m == 0 and t == 0), stop=(m == DT - 1 and t == TT - 1))
                    elif kind == "Z":
                        if g == 1 and i == 0:
                            pe.wait_ge(s_read, emptied(job(c, 1, "DTT", 0)))
                        j = ng * Q + i
                        last = pe.matmul(pX[:], wdt[:, j * P:(j + 1) * P], dtT[:],
                                         start=True, stop=True)
                    else:
                        if kind == "XT" and i == 0:
                            pe.wait_ge(s_xn, (cc + 1) * TT)
                        if kind == "YT" and i == 0:
                            pe.wait_ge(s_stt, of_phase(ph - 1, N - 1, TT - 1, TT) + RING)
                        if kind == "UD":
                            pe.wait_ge(s_ud, (ph + 1) * Q + i + 1)
                        if kind == "DTT":
                            pe.wait_ge(s_ssn, (cc + 1) * 3)
                            pe.wait_ge(s_dts, (cc + 1) * 3)
                        plain(pe)
                        for t in range(TT):
                            ts = slice(t * P, (t + 1) * P)
                            if kind == "XT":
                                last = pe.transpose(pX[:, ts], xn[:, t, i * P:(i + 1) * P], ident[:])
                            elif kind == "YT":
                                last = pe.transpose(pX[:, ts], yT[:, ng, t, i * P:(i + 1) * P], ident[:])
                            elif kind == "UD":
                                last = pe.transpose(pX[:, ts], ud[:, i % 2, ts], ident[:])
                            elif kind == "DTT":
                                last = pe.transpose(pX[0:DTR + N, ts], dts[:, t], ident[:])
                    if part == parts - 1:
                        last.then_inc(s_full, 1)

                if isinstance(c, int) and (c, g) == (-1, 1):
                    pe.wait_ge(s_const, 16 * len(consts))
                    pe.wait_ge(s_wdt, 3)
                if isinstance(c, int) and (c, g) == (0, 0):
                    pe.wait_ge(s_read, emptied(job(0, 0, "GT", 0) - 1))
                for n in range(N):
                    for q in range(Q):
                        if n == 0 and scan_before(c, g) and q < 3:
                            turn_h(ph - 1, N - 1, q + 1)
                        if n >= 1 and scan and q < 3:
                            turn_h(ph, n - 1, q + 1)
                        if scan and q == 3:
                            turn_h(ph, n, 0)
                        if scan:
                            if q == 0 and 2 <= n < MT + 2:
                                down(n - 2)
                            if q == 1 and n == 0:
                                pe.wait_ge(s_xlo, (c + 1) * 2)
                            if 1 <= q <= 2 and n < MT:
                                up(n, q - 1)
                        for kind, i, q0, q1 in at_quarter(g, n, q):
                            if q0 <= q <= q1:
                                k = job(c, g, kind, i)
                                if q == q0 and not alone(c):
                                    pe.wait_ge(s_read, emptied(k - 1))
                                if q == q0 and alone(c) and k >= 2:
                                    pe.wait_ge(s_read, emptied(k - 2))
                                if does(kind, post, work, ahead):
                                    side(kind, i, k, q - q0, q1 - q0 + 1)
                                elif q == q1:
                                    if alone(c) and k >= 1:
                                        pe.wait_ge(s_full, filled(k - 1))
                                    pe.sem_inc(s_full, 1)
                                    if not alone(c):
                                        pe.sem_inc(s_read, 1)
                plain(pe)
            phases(pe, phase)


def kernel(**inputs):
    import numpy as np
    import concourse.bacc as bacc
    from concourse.bass_utils import run_bass_kernel_spmd as run

    a = {k.replace("L0_", ""): np.asarray(v) for k, v in inputs.items()}

    def tiles(w, n):
        return w.reshape(n, P, -1).transpose(1, 0, 2)

    w_in = a["attn_W_in"].reshape(2, DT, P, HT, P).transpose(1, 0, 4, 3, 2)
    w_gu = np.stack([a["ffn_W_gate"], a["ffn_W_up"]]).reshape(2, MT, P, HT, P).transpose(1, 4, 0, 3, 2)
    arrays = {
        "x": a["attn_hidden_states"].reshape(CHUNKS, TT, P, H).transpose(0, 2, 1, 3),
        "w_in": w_in,
        "conv_w": tiles(a["attn_conv_w"], DT),
        "conv_b": a["attn_conv_b"].reshape(DT, P).T,
        "w_x": tiles(a["attn_Wx"].T, DT),
        "dt_ln": a["attn_dt_ln_w"], "b_ln": a["attn_b_ln_w"], "c_ln": a["attn_c_ln_w"],
        "w_dt": a["attn_Wdt"].T,
        "dt_bias": a["attn_dt_bias"].reshape(DT, P).T,
        "a_mat": tiles(a["attn_A"], DT),
        "d_par": a["attn_D_param"].reshape(DT, P).T,
        "w_out": tiles(a["attn_W_out"].T, DT),
        "w_gu": w_gu,
        "w_dn": tiles(a["ffn_W_down"].T, MT).reshape(P, MT * H),
    }
    arrays = {k: np.ascontiguousarray(v) for k, v in arrays.items()}
    nc = bacc.Bacc("TRN2", target_bir_lowering=False, num_devices=1)
    aps = {k: nc.dram_tensor(k, v.shape, mybir.dt.from_np(v.dtype), kind="ExternalInput").ap()
           for k, v in arrays.items()}
    aps["b_rows"] = nc.dram_tensor("b_rows", (CHUNKS, N, T), F32, kind="Internal").ap()
    aps["wdn_rows"] = nc.dram_tensor("wdn_rows", (MT, P, H), F32, kind="Internal").ap()
    aps["out"] = nc.dram_tensor("out", (CHUNKS, P, TT, H), F32, kind="ExternalOutput").ap()
    build(nc, **aps)
    got = run(nc, [arrays], core_ids=[0]).results[0]["out"]
    return got.transpose(0, 2, 1, 3).reshape(BATCH, SEQ, H)
```
